# Optimizing a Trainium2 kernel written in Bass

```python
import numpy as np
import jax
import jax.numpy as jnp

def _softmax(x, axis=-1):
    return jax.nn.softmax(x, axis=axis)
def _gelu(x):
    return jax.nn.gelu(x, approximate=True)
def _silu(x):
    return jax.nn.silu(x)
def _sigmoid(x):
    return jax.nn.sigmoid(x)
def _layernorm(x, axis=-1, eps=1e-5):
    m = jnp.mean(x, axis=axis, keepdims=True)
    v = jnp.var(x, axis=axis, keepdims=True)
    return (x - m) / jnp.sqrt(v + eps)
def _scatter_add(tgt, idx, src, axis=0):
    return tgt.at[idx].add(src)
def _segment_sum(src, seg, n):
    return jax.ops.segment_sum(src, seg, n)

kernel_name = 'mk_metaformer_d1_conv_nhwc128_33ce8d'

def setup_inputs(seed: int = 0):
    np.random.seed(seed)
    _w = jnp.asarray
    def _rec_inputs():
        import jax
        import jax.numpy as jnp
        _gk = jax.random.key(seed)
        x = -0.0004039 + 1 * jax.random.normal(jax.random.fold_in(_gk, 1), (4, 192, 128, 128), jnp.float32)
        return x
    x = _rec_inputs()
    def _L0_conv_setup():
        import jax, jax.numpy as jnp
        import numpy as np
        B, C, H, W = (4, 192, 128, 128)
        HEADS, QK_DIM = (6, 192)
        DH, DW = (16, 16)
        STEP_H, STEP_W = (DH - 2, DW - 2)
        EPS = 1e-05

        def _starts(size, step, win):
            return np.array([min(i, size - win) for i in range(0, size + step - win, step)], dtype=np.int64)
        TOPS = _starts(H, STEP_H, DH)
        LEFTS = _starts(W, STEP_W, DW)
        NH, NW = (len(TOPS), len(LEFTS))
        N = NH * NW
        ROW = TOPS[:, None] + np.arange(DH)
        COL = LEFTS[:, None] + np.arange(DW)
        COUNT = np.zeros((H, W), dtype=np.float32)
        for t in TOPS:
            for l in LEFTS:
                COUNT[t:t + DH, l:l + DW] += 1.0
        COUNT = jnp.asarray(COUNT)
        key = jax.random.key(seed)
        ks = jax.random.split(key, 4)
        x = jax.random.normal(ks[0], (B, C, H, W), dtype=jnp.float32)
        Wq = jax.random.normal(ks[1], (QK_DIM, C), dtype=jnp.float32) * 0.02
        Wk = jax.random.normal(ks[2], (QK_DIM, C), dtype=jnp.float32) * 0.02
        Wv = jax.random.normal(ks[3], (C, C), dtype=jnp.float32) * 0.02
        ln_gamma = jnp.ones((C,), dtype=jnp.float32)
        ln_beta = jnp.zeros((C,), dtype=jnp.float32)
        return {'x': x, 'Wq': Wq, 'Wk': Wk, 'Wv': Wv, 'ln_gamma': ln_gamma, 'ln_beta': ln_beta}
    _L0_conv_all = _L0_conv_setup()
    _L0_conv_in = {k: v for k, v in _L0_conv_all.items() if k in ('Wq', 'Wk', 'Wv', 'ln_gamma', 'ln_beta', )}
    del _L0_conv_all

    def _L0_ffn_setup():
        import jax, jax.numpy as jnp
        import numpy as np
        B, N, D, C, E, K = (8, 8192, 128, 128, 8, 2)
        key = jax.random.key(seed)
        k0, k1, k2 = jax.random.split(key, 3)
        x = jax.random.normal(k0, (B, N, D), dtype=jnp.float32)
        router_w = jax.random.normal(k1, (D, E), dtype=jnp.float32) * 0.05
        router_b = jnp.zeros((E,), dtype=jnp.float32)
        expert_w = jax.random.normal(k2, (E, D, C), dtype=jnp.float32) * (1.0 / np.sqrt(D))
        expert_b = jnp.zeros((E, C), dtype=jnp.float32)
        return {'x': x, 'router_w': router_w, 'router_b': router_b, 'expert_w': expert_w, 'expert_b': expert_b}
    _L0_ffn_all = _L0_ffn_setup()
    _L0_ffn_in = {k: v for k, v in _L0_ffn_all.items() if k in ('router_w', 'router_b', 'expert_w', 'expert_b', )}
    del _L0_ffn_all

    return {
        "x": x,
        "L0_conv_Wq": _L0_conv_in["Wq"],
        "L0_conv_Wk": _L0_conv_in["Wk"],
        "L0_conv_Wv": _L0_conv_in["Wv"],
        "L0_conv_ln_gamma": _L0_conv_in["ln_gamma"],
        "L0_conv_ln_beta": _L0_conv_in["ln_beta"],
        "L0_ffn_router_w": _L0_ffn_in["router_w"],
        "L0_ffn_router_b": _L0_ffn_in["router_b"],
        "L0_ffn_expert_w": _L0_ffn_in["expert_w"],
        "L0_ffn_expert_b": _L0_ffn_in["expert_b"],
    }

def reference(x, L0_conv_Wq, L0_conv_Wk, L0_conv_Wv, L0_conv_ln_gamma, L0_conv_ln_beta, L0_ffn_router_w, L0_ffn_router_b, L0_ffn_expert_w, L0_ffn_expert_b):
    import jax
    import jax.numpy as jnp
    def _L0_conv_ref(x, Wq, Wk, Wv, ln_gamma, ln_beta):
        import jax, jax.numpy as jnp
        import numpy as np
        B, C, H, W = (4, 192, 128, 128)
        HEADS, QK_DIM = (6, 192)
        DH, DW = (16, 16)
        STEP_H, STEP_W = (DH - 2, DW - 2)
        EPS = 1e-05

        def _starts(size, step, win):
            return np.array([min(i, size - win) for i in range(0, size + step - win, step)], dtype=np.int64)
        TOPS = _starts(H, STEP_H, DH)
        LEFTS = _starts(W, STEP_W, DW)
        NH, NW = (len(TOPS), len(LEFTS))
        N = NH * NW
        ROW = TOPS[:, None] + np.arange(DH)
        COL = LEFTS[:, None] + np.arange(DW)
        COUNT = np.zeros((H, W), dtype=np.float32)
        for t in TOPS:
            for l in LEFTS:
                COUNT[t:t + DH, l:l + DW] += 1.0
        COUNT = jnp.asarray(COUNT)
        r = ROW[:, None, :, None]
        c = COL[None, :, None, :]
        win = x[:, :, r, c]
        lx = win.transpose(0, 2, 3, 4, 5, 1)
        lx = lx.reshape(B * N, DH * DW, C)
        mu = jnp.mean(lx, axis=-1, keepdims=True)
        var = jnp.mean((lx - mu) ** 2, axis=-1, keepdims=True)
        lx = (lx - mu) * jax.lax.rsqrt(var + EPS) * ln_gamma + ln_beta
        q = jnp.einsum('bsc,qc->bsq', lx, Wq)
        k = jnp.einsum('bsc,qc->bsq', lx, Wk)
        v = jnp.einsum('bsc,vc->bsv', lx, Wv)
        S = DH * DW
        dq = QK_DIM // HEADS
        dv = C // HEADS
        q = q.reshape(B * N, S, HEADS, dq).transpose(0, 2, 1, 3)
        k = k.reshape(B * N, S, HEADS, dq).transpose(0, 2, 1, 3)
        v = v.reshape(B * N, S, HEADS, dv).transpose(0, 2, 1, 3)
        scale = QK_DIM ** (-0.5)
        attn = jnp.einsum('bhsd,bhtd->bhst', q, k) * scale
        attn = jax.nn.softmax(attn, axis=-1)
        out = jnp.einsum('bhst,bhtd->bhsd', attn, v)
        out = out.transpose(0, 2, 1, 3).reshape(B * N, S, C)
        out = out.reshape(B, NH, NW, DH, DW, C).transpose(0, 5, 1, 2, 3, 4)
        acc = jnp.zeros_like(x).at[:, :, r, c].add(out)
        return acc / COUNT[None, None]

    def _L0_ffn_ref(x, router_w, router_b, expert_w, expert_b):
        import jax, jax.numpy as jnp
        import numpy as np
        B, N, D, C, E, K = (8, 8192, 128, 128, 8, 2)
        router_probs = jax.nn.softmax(x @ router_w + router_b, axis=-1)
        top_p, top_i = jax.lax.top_k(router_probs, K)
        top_p = top_p / jnp.sum(top_p, axis=-1, keepdims=True)
        expert_out = jnp.einsum('bnd,edc->bnec', x, expert_w) + expert_b
        gathered = jnp.take_along_axis(expert_out, top_i[..., None], axis=2)
        return jnp.einsum('bnk,bnkc->bnc', top_p, gathered)

    def _gn(v, G=32, eps=1e-5):
        B_, H_, W_, C_ = v.shape
        g = v.reshape(B_, H_, W_, G, C_ // G)
        m = jnp.mean(g, axis=(1, 2, 4), keepdims=True)
        s = jnp.var(g, axis=(1, 2, 4), keepdims=True)
        return ((g - m) / jnp.sqrt(s + eps)).reshape(v.shape)

    def _ln_c(v, eps=1e-6):
        m = jnp.mean(v, axis=-1, keepdims=True)
        s = jnp.var(v, axis=-1, keepdims=True)
        return (v - m) / jnp.sqrt(s + eps)

    def _ln_t(v, eps=1e-5):
        m = jnp.mean(v, axis=-1, keepdims=True)
        s = jnp.var(v, axis=-1, keepdims=True)
        return (v - m) / jnp.sqrt(s + eps)

    def _to_tokens(v):
        B_, H_, W_, C_ = v.shape
        return v.reshape(B_, H_ * W_, C_)
    def _from_tokens(t, like):
        return t.reshape(like.shape)

    x = x + _L0_conv_ref(_ln_c(x), L0_conv_Wq, L0_conv_Wk, L0_conv_Wv, L0_conv_ln_gamma, L0_conv_ln_beta)
    t = _to_tokens(x)
    t = t + _L0_ffn_ref(_ln_t(t), L0_ffn_router_w, L0_ffn_router_b, L0_ffn_expert_w, L0_ffn_expert_b)
    x = _from_tokens(t, x)
    return x


_drawn_inputs = setup_inputs


def setup_inputs(seed=0):
    import zlib

    import numpy as np

    out = dict(_drawn_inputs(seed))
    spreads = {'L0_conv_ln_gamma': (1.0, 0.2),
     'L0_conv_ln_beta': (0.0, 0.329),
     'L0_ffn_router_b': (0.0, 0.1),
     'L0_ffn_expert_b': (0.0, 0.1)}
    factors = {'L0_conv_Wq': 4.171, 'L0_conv_Wk': 4.371}
    for name, (base, spread) in spreads.items():
        noise = np.random.default_rng([zlib.crc32(name.encode()), seed]).standard_normal(out[name].shape)
        drawn = base * np.exp(spread * noise) if base else spread * noise
        out[name] = jnp.asarray(drawn.astype(out[name].dtype))
    for name, factor in factors.items():
        out[name] = (out[name] * factor).astype(out[name].dtype)
    return out
```

```python
from contextlib import ExitStack

import concourse.bass as bass
from concourse import mybir

F32 = mybir.dt.float32
F32R = mybir.dt.float32r
ACT = mybir.ActivationFunctionType
ALU = mybir.AluOpType
AX = mybir.AxisListType

B, C, H, W = 4, 192, 128, 128
HEADS = 6
HD = C // HEADS
CH = 96
NCH = C // CH
HC = CH // HD
WIN, STEP = 16, 14
NWIN = (H - WIN) // STEP + 1
BANDS = B * NWIN
SEQ = WIN * WIN
BODY = 2 * NWIN
TURNS = BANDS // 2
QROWS = 4
SCALE = float(C) ** -0.5
EPS_ROW, EPS_PIX = 1e-6, 1e-5

ROW_AT, TURN_AT, BACK_AT = 1, 2, 3

JOBS = ("max_rows", "back0", "back1", "qk01", "turn0", "turn1", "qk2", "v")
PSUM_SLOTS = 2

RSTD_STEPS = 9
EDGE = 2 * WIN
STEPS_A_TURN = 2 * (QROWS * (2 * RSTD_STEPS + 1) + 3 * NWIN + 2 + NCH)


def groups_beside(k, first):
    q = k % NWIN - first
    return q if 0 <= q < QROWS else None


def jobs_beside(k):
    out = []
    for name in JOBS:
        if name.startswith("back") and groups_beside(k, BACK_AT) is None:
            continue
        if name.startswith("turn") and groups_beside(k, TURN_AT) is None:
            continue
        out.append(name)
    return out


def job_table():
    table, n = {}, 0
    for q in range(QROWS):
        for name in ("turn0", "turn1", "back0", "back1"):
            table[("prep", q, name)] = n
            n += 1
    for k in (-3, -2, -1):
        for name in (("max_rows",) if k == -1 else ()) + ("qk01", "qk2", "v"):
            table[(k, name)] = n
            n += 1
    ahead = n
    for k in range(BODY):
        for name in jobs_beside(k):
            table[(k, name)] = n
            n += 1
    assert ahead % PSUM_SLOTS == 0 and (n - ahead) % PSUM_SLOTS == 0
    return table, (n - ahead) // PSUM_SLOTS


JOB, JOBS_A_TURN = job_table()


def wait(engine, sem, value):
    if isinstance(value, int) and value <= 0:
        return
    engine.wait_ge(sem, value)


def wait_alone(engine, sem, value):
    if not isinstance(value, int):
        value = engine.to_reg(value)
        engine.wait_ge(sem, 1)
    engine.wait_ge(sem, value)


def rstd(pool, done, settle, stats, tmp, count, eps, scale_out, shift_out, minus_half):
    total, diff, spread = tmp
    done(pool.tensor_tensor(total, stats[:, :, 1], stats[:, :, 4], ALU.add))
    done(pool.tensor_tensor(diff, stats[:, :, 1], stats[:, :, 4], ALU.subtract))
    done(pool.tensor_tensor(spread, stats[:, :, 2], stats[:, :, 5], ALU.add))
    settle()
    done(pool.tensor_tensor(diff, diff, diff, ALU.mult))
    done(pool.tensor_scalar(spread, spread, 4.0 / count, 0.0, ALU.mult, ALU.add))
    settle()
    done(pool.tensor_tensor(diff, diff, spread, ALU.add))
    settle(True)
    done(pool.tensor_scalar(diff, diff, 0.25, eps, ALU.mult, ALU.add))
    settle()
    done(pool.tensor_tensor(scale_out, diff, minus_half, ALU.pow))
    settle()
    done(pool.tensor_tensor(spread, total, scale_out, ALU.mult))
    settle(True)
    return pool.tensor_scalar(shift_out, spread, -0.5, 0.0, ALU.mult, ALU.add)


def attention(nc, x, wq, wk, wv, gamma, beta, x2, turns=TURNS):
    x_v = x.rearrange("b (n c) h w -> b c n (h w)", n=NCH)
    x2_v = x2.rearrange("b (n c) h w -> b c n (h w)", n=NCH)

    with ExitStack() as ctx:
        def sb(name, shape, dt=F32):
            return ctx.enter_context(nc.sbuf_tensor(name, shape, dt))

        def sem(name):
            return ctx.enter_context(nc.semaphore(name))

        acc = sb("acc", [CH, 2, NCH, WIN * W])
        y = sb("y", [CH, 2, NCH, QROWS, W])
        y_pix = sb("y_pix", [W, 2, QROWS, C])
        z_hi = sb("z_hi", [CH, 2, NCH, NWIN, SEQ], F32R)
        z_lo = sb("z_lo", [CH, 2, NCH, NWIN, SEQ], F32R)
        nat = sb("nat", [128, 2, 2, 3, SEQ], F32R)
        st = [sb(f"st{i}", [CH + 1, 2 * HEADS, SEQ], F32R) for i in range(3)]
        v_sb = sb("v_sb", [128, 3, 2, C])
        prob = sb("prob", [128, HEADS, 2 * SEQ])
        rinv = sb("rinv", [CH, NCH * SEQ])
        o_sb = sb("o_sb", [CH, 2, NCH, SEQ])
        neg_max = sb("neg_max", [128, 2, 2 * HEADS])
        max_rows = sb("max_rows", [2 * HEADS, 2, 128], F32R)
        row_stats = sb("row_stats", [CH, 2, NCH * QROWS, 6])
        row_tmp = sb("row_tmp", [CH, 6, NCH * QROWS])
        pix_stats = sb("pix_stats", [W, 2, QROWS, 6])
        pix_tmp = sb("pix_tmp", [W, 4, QROWS])
        pix_scale = sb("pix_scale", [W, 2, 2, QROWS])
        minus_half = sb("minus_half", [128, NCH * QROWS])
        wqk_hi = sb("wqk_hi", [CH, NCH, 3 * 128], F32R)
        wqk_lo = sb("wqk_lo", [CH, NCH, 3 * 128], F32R)
        wv_hi = sb("wv_hi", [CH, NCH, SEQ], F32R)
        wv_lo = sb("wv_lo", [CH, NCH, SEQ], F32R)
        qk_bias = sb("qk_bias", [128, 3])
        v_bias = sb("v_bias", [128, C])
        ident = sb("ident", [128, 128])
        ones = sb("ones", [128, HD])
        one_half = sb("one_half", [CH, 2 * EDGE])
        edge_weight = sb("edge_weight", [CH, 2, EDGE])
        gb = sb("gb", [CH, 2, NCH])

        ps_s = [ctx.enter_context(nc.psum_tensor(f"ps_s{i}", [128, 512], F32)) for i in range(2)]
        ps_t = [ctx.enter_context(nc.psum_tensor(f"ps_t{i}", [128, 512], F32)) for i in range(2)]
        ps_w = [ctx.enter_context(nc.psum_tensor(f"ps_w{i}", [128, 512], F32)) for i in range(2)]
        ps_o = ctx.enter_context(nc.psum_tensor("ps_o", [128, 512], F32))
        ps_r = ctx.enter_context(nc.psum_tensor("ps_r", [128, 512], F32))

        raw = prob[0:CH, :, :].rearrange("p a b -> p (a b)")
        w_raw = raw[:, 0:3 * NCH * C].rearrange("p (t n c) -> p t n c", t=3, n=NCH)
        w_t = raw[:, 3 * NCH * C:6 * NCH * C].rearrange("p (t n q) -> p t n q", t=3, n=NCH)
        w_slot = raw[:, 6 * NCH * C:6 * NCH * C + NCH * 384].rearrange("p (n q) -> p n q", n=NCH)
        scaled = y[:, 0, :, :, :].rearrange("p n r w -> p (n r w)")[:, 0:NCH * 384].rearrange(
            "p (n q) -> p n q", n=NCH)
        scaled_v = y[:, 1, :, :, :].rearrange("p n r w -> p (n r w)")[:, 0:NCH * C].rearrange(
            "p (n q) -> p n q", n=NCH)
        beta_wide = o_sb[:, 0, :, 0:128]

        w_in = sem("w_in")
        const = sem("const")
        w_turned = sem("w_turned")
        w_copied = sem("w_copied")
        w_step = sem("w_step")
        bias_ready = sem("bias_ready")

        with nc.Block() as block:
            @block.sync
            def _(sp):
                for t, w in enumerate((wq, wk, wv)):
                    sp.dma_start(w_raw[:, t, :, :], w.rearrange("(n p) c -> p n c", n=NCH)).then_inc(w_in, 16)
                for t, w in enumerate((gamma, beta)):
                    for n in range(NCH):
                        sp.dma_start(gb[:, t, n:n + 1], w[n * CH:(n + 1) * CH].rearrange("(p a) -> p a", a=1)
                                     ).then_inc(w_in, 16)

            @block.gpsimd
            def _(pool):
                pool.memset(ident[:], 0.0).then_inc(const, 1)
                pool.memset(ones[:], 1.0).then_inc(const, 1)
                pool.memset(minus_half[:], -0.5).then_inc(const, 1)
                pool.memset(one_half[:, 0:EDGE], 1.0).then_inc(const, 1)
                pool.memset(one_half[:, EDGE:], 0.5).then_inc(const, 1)
                pool.memset(wv_hi[:].bitcast(F32), 0.0).then_inc(const, 1)
                pool.memset(wv_lo[:].bitcast(F32), 0.0).then_inc(const, 1)
                pool.wait_ge(const, 7)
                pool.affine_select(out=ident[:], in_=ident[:], compare_op=ALU.not_equal, fill=1.0, base=0,
                                   pattern=[[-1, 128]], channel_multiplier=1).then_inc(const, 1)

            @block.tensor
            def _(pe):
                pe.wait_ge(const, 8)
                pe.wait_ge(w_in, 16 * (3 + 2 * NCH))
                for t, bank in enumerate((ps_s[0], ps_s[1], ps_t[0])):
                    for n in range(NCH):
                        for qn in range(NCH):
                            last = pe.transpose(bank[0:CH, n * C + qn * CH:n * C + (qn + 1) * CH],
                                                w_raw[:, t, qn, n * CH:(n + 1) * CH], ident[0:CH, 0:CH])
                    last.then_inc(w_turned, 1)
                pe.wait_ge(w_step, 3)
                for c in range(3):
                    for n in range(NCH):
                        pe.matmul(ps_t[1][:, c:c + 1], w_slot[:, n, c * 128:(c + 1) * 128], gb[:, 1, n:n + 1],
                                  start=(n == 0), stop=(n == NCH - 1))
                for n in range(NCH):
                    last = pe.matmul(ps_w[0][:, 0:C], beta_wide[:, n, :], w_t[:, 2, n, :],
                                     start=(n == 0), stop=(n == NCH - 1))
                last.then_inc(bias_ready, 1)

            @block.vector
            def _(dve):
                for slot in st:
                    dve.memset(slot[CH:CH + 1, :, :].bitcast(F32), 1.0)
                for t, bank in enumerate((ps_s[0], ps_s[1], ps_t[0])):
                    dve.wait_ge(w_turned, t + 1)
                    dve.tensor_copy(w_t[:, t, :, :], bank[0:CH, 0:NCH * C].rearrange("p (n q) -> p n q", n=NCH)
                                    ).then_inc(w_copied, 1)
                dve.wait_ge(w_copied, 3)
                for t in range(2):
                    for n in range(NCH):
                        last = dve.tensor_copy(
                            w_slot[:, n, :].rearrange("p (c b d) -> p b c d", c=3, b=4)[:, 2 * t:2 * t + 2],
                            w_t[:, t, n, :].rearrange("p (b c d) -> p b c d", b=2, c=3))
                last.then_inc(w_step, 1)
                dve.tensor_copy(beta_wide, gb[:, 1, :].unsqueeze(2).broadcast_to([CH, NCH, 128])
                                ).then_inc(w_step, 1)
                dve.wait_ge(w_step, 2)
                for n in range(NCH):
                    dve.tensor_scalar(scaled[:, n, :], w_slot[:, n, :], gb[:, 0, n:n + 1], None, ALU.mult)
                    last = dve.tensor_scalar(scaled_v[:, n, :], w_t[:, 2, n, :], gb[:, 0, n:n + 1], None, ALU.mult)
                last.then_inc(w_step, 1)
                dve.wait_ge(w_step, 3)
                dve.wait_ge(const, 8)
                dve.tensor_copy(wqk_hi[:], scaled)
                dve.tensor_copy(wv_hi[:, :, 0:C], scaled_v).then_inc(w_step, 1)
                dve.wait_ge(w_step, 4)
                dve.tensor_tensor(wqk_lo[:], scaled, wqk_hi[:].bitcast(F32), ALU.subtract)
                dve.tensor_tensor(wv_lo[:, :, 0:C], scaled_v, wv_hi[:, :, 0:C].bitcast(F32), ALU.subtract)
                dve.wait_ge(bias_ready, 1)
                dve.tensor_copy(qk_bias[:], ps_t[1][:, 0:3])
                dve.tensor_copy(v_bias[:], ps_w[0][:, 0:C]).then_inc(w_step, 1)

        x_in = [sem(f"x_in{p}") for p in range(2)]
        row_counts = sem("row_counts")
        y_ready = sem("y_ready")
        pix_counts = sem("pix_counts")
        pix_ready = sem("pix_ready")
        pix_done = sem("pix_done")
        z_hi_done = sem("z_hi_done")
        qk_hi_done = sem("qk_hi_done")
        w_full = [sem(f"w_full{i}") for i in range(2)]
        w_free = [sem(f"w_free{i}") for i in range(2)]
        st_in = [sem(f"st_in{i}") for i in range(3)]
        s_full = sem("s_full")
        s_maxed = [sem(f"s_maxed{i}") for i in range(2)]
        max_in = sem("max_in")
        t_full = sem("t_full")
        exp_done = [sem(f"exp_done{i}") for i in range(2)]
        pv_done = [sem(f"pv_done{i}") for i in range(2)]
        ln_done = sem("ln_done")
        rinv_ready = sem("rinv_ready")
        o_ready = sem("o_ready")
        added = [sem(f"added{i}") for i in range(2)]
        pool_step = sem("pool_step")
        stored = [sem(f"stored{p}") for p in range(2)]

        def job(key, turn):
            n = JOB[key]
            return n % 2, n // 2 if key[0] == "prep" else n // 2 + turn * JOBS_A_TURN

        def pe_steps(pe):
            def scores(turn, k, h):
                v = BODY * turn + k
                slot = st[k % 3]
                if h == 0:
                    wait(pe, st_in[k % 3], 192 * (6 * turn + k // 3 + 1))
                wait(pe, s_maxed[h % 2], 3 * v + h // 2)
                for half in range(2):
                    mm = pe.matmul(ps_s[h % 2][:, half * SEQ:(half + 1) * SEQ],
                                   slot[0:CH, h, half * 128:(half + 1) * 128], slot[0:CH, HEADS + h, :],
                                   start=True, stop=True)
                mm.then_inc(s_full, 1)

            def scores_t(turn, k, h):
                v = BODY * turn + k
                slot = st[k % 3]
                if h == 0:
                    pe.wait_ge(max_in, 16 * (v + 1))
                wait(pe, exp_done[h % 2], 3 * v + h // 2)
                for half in range(2):
                    mm = pe.matmul(ps_t[h % 2][:, half * SEQ:(half + 1) * SEQ],
                                   slot[:, HEADS + h, half * 128:(half + 1) * 128], slot[:, h, :],
                                   start=True, stop=True)
                mm.then_inc(t_full, 1)

            def weigh(turn, k, n):
                v = BODY * turn + k
                for h in (HC * n, HC * n + 1, HC * n + 2):
                    wait(pe, exp_done[h % 2], 3 * v + h // 2 + 1)
                if n == 0:
                    wait(pe, o_ready, v)
                    wait(pe, ln_done, v)
                for half in range(2):
                    for bank, weights in ((ps_o, None), (ps_r, ones)):
                        for a in range(HC):
                            h = HC * n + a
                            lhs = ones[:] if weights is not None else v_sb[:, k % 3, half, h * HD:(h + 1) * HD]
                            mm = pe.matmul(bank[a * HD:(a + 1) * HD, n * SEQ:(n + 1) * SEQ], lhs,
                                           prob[:, h, half * SEQ:(half + 1) * SEQ],
                                           start=(half == 0), stop=(half == 1), tile_position=(0, a * HD))
                mm.then_inc(pv_done[n], 1)

            def take(key, turn):
                bank, before = job(key, turn)
                wait(pe, w_free[bank], before)
                return bank, ps_w[bank]

            def max_turn(key, turn, k):
                v = BODY * turn + k
                bank, ps = take(key, turn)
                for i in range(2):
                    pe.wait_ge(s_maxed[i], 3 * (v + 1))
                pe.transpose(ps[0:2 * HEADS, 0:128], neg_max[:, k % 2, :], ident[:]).then_inc(w_full[bank], 1)

            def turn_rows(key, turn, group, par, half):
                bank, ps = take(key, turn)
                if half == 0:
                    pe.wait_ge(y_ready, group + 1)
                for r in range(2):
                    for n in range(NCH):
                        mm = pe.transpose(ps[:, r * C + n * CH:r * C + (n + 1) * CH],
                                          y[:, par, n, 2 * half + r, :], ident[0:CH, 0:CH])
                mm.then_inc(w_full[bank], 1)

            def turn_back(key, turn, group, par, half):
                bank, ps = take(key, turn)
                pe.wait_ge(pix_done, QROWS * group + 2 * half + 2)
                for n in range(NCH):
                    for r in range(2):
                        mm = pe.transpose(ps[0:CH, (2 * n + r) * W:(2 * n + r + 1) * W],
                                          y_pix[:, par, 2 * half + r, n * CH:(n + 1) * CH], ident[:])
                mm.then_inc(w_full[bank], 1)

            def project(key, turn, k, chunks):
                par, w = k // NWIN % 2, k % NWIN
                bank, ps = take(key, turn)
                for i, c in enumerate(chunks):
                    parts = [(a, z, n) for a, z in ((wqk_hi, z_hi), (wqk_hi, z_lo), (wqk_lo, z_hi))
                             for n in range(NCH)]
                    for j, (a, z, n) in enumerate(parts):
                        mm = pe.matmul(ps[:, i * SEQ:(i + 1) * SEQ], a[:, n, c * 128:(c + 1) * 128],
                                       z[:, par, n, w, :], start=(j == 0), stop=(j == len(parts) - 1))
                mm.then_inc(w_full[bank], 1)

            def project_v(key, turn, k):
                par, w = k // NWIN % 2, k % NWIN
                bank, ps = take(key, turn)
                for half in range(2):
                    parts = [(a, z, n) for a, z in ((wv_hi, z_hi), (wv_hi, z_lo), (wv_lo, z_hi))
                             for n in range(NCH)]
                    for j, (a, z, n) in enumerate(parts):
                        mm = pe.matmul(ps[:, half * SEQ:(half + 1) * SEQ],
                                       z[:, par, n, w, half * 128:(half + 1) * 128], a[:, n, :],
                                       start=(j == 0), stop=(j == len(parts) - 1))
                mm.then_inc(w_full[bank], 1)

            return scores, scores_t, weigh, max_turn, turn_rows, turn_back, project, project_v

        def by_window(ps):
            def of(n):
                t = ps[0:CH, 2 * n * W:(2 * n + 2) * W].rearrange("p (r w) -> p r w", r=2)
                return overlapped(t)
            return of

        def overlapped(t):
            part, row = list(t.ap[0]), list(t.ap[1])
            return bass.AP(tensor=t.tensor, offset=t.offset, ap=[part, [STEP, NWIN], row, [1, WIN]])

        def z_rows(z, zpar, n, q, half):
            r = QROWS * q + 2 * half
            return z[:, zpar, n, :, r * WIN:(r + 2) * WIN].rearrange("p v (r c) -> p v r c", r=2)

        def next_group(turn, k, q):
            return 2 * QROWS * turn + QROWS * (k // NWIN + 1) + q, q % 2

        with nc.Block() as block:
            @block.tensor
            def _(pe):
                (scores, scores_t, weigh, max_turn, turn_rows, turn_back, project, project_v) = pe_steps(pe)

                def project_window(turn, k, key_k, name):
                    if name == "v":
                        project_v((key_k, name), turn, k)
                    else:
                        project((key_k, name), turn, k, (0, 1) if name == "qk01" else (2,))

                def z_complete(key, turn):
                    bank, before = job(key, turn)
                    pe.wait_ge(w_free[bank], before + 1)

                for q in range(QROWS):
                    for half in range(2):
                        turn_rows(("prep", q, f"turn{half}"), 0, q, q % 2, half)
                    for half in range(2):
                        turn_back(("prep", q, f"back{half}"), 0, q, q % 2, half)
                z_complete(("prep", QROWS - 1, "back1"), 0)
                for k in (-3, -2, -1):
                    if k == -1:
                        for h in range(HEADS):
                            scores(0, 0, h)
                        max_turn((k, "max_rows"), 0, 0)
                    for name in ("qk01", "qk2", "v"):
                        project_window(0, k + 3, k, name)

                with pe.Fori(0, turns) as turn:
                    for k in range(BODY):
                        def sc(h, turn=turn, k=k):
                            scores(turn, k + 1, h)

                        def sct(h, turn=turn, k=k):
                            scores_t(turn, k, h)
                        back, rows = groups_beside(k, BACK_AT), groups_beside(k, TURN_AT)
                        sc(0), sc(1), sct(0), sc(2), sct(1), sc(3), sct(2), sc(4), sct(3), sc(5), sct(4)
                        weigh(turn, k, 0)
                        sct(5)
                        max_turn((k, "max_rows"), turn, k + 1)
                        if back is not None:
                            group, par = next_group(turn, k, back)
                            for half in range(2):
                                turn_back((k, f"back{half}"), turn, group, par, half)
                        weigh(turn, k, 1)
                        if k % NWIN == NWIN - 3:
                            z_complete((k, "back1"), turn)
                        project_window(turn, k + 3, k, "qk01")
                        if rows is not None:
                            group, par = next_group(turn, k, rows)
                            for half in range(2):
                                turn_rows((k, f"turn{half}"), turn, group, par, half)
                        project_window(turn, k + 3, k, "qk2")
                        project_window(turn, k + 3, k, "v")

            @block.scalar
            def _(act):
                act.preload_act_table_set("natural_log_exp_and_others")

                def full(key, turn):
                    bank, before = job(key, turn)
                    act.wait_ge(w_full[bank], before + 1)
                    return bank, ps_w[bank]

                def exponentials(turn, k, h):
                    v = BODY * turn + k
                    act.wait_ge(t_full, HEADS * v + h + 1)
                    wait(act, pv_done[h // HC], v)
                    act.activation(prob[:, h, :], ps_t[h % 2][:], ACT.Exp, scale=SCALE
                                   ).then_inc(exp_done[h % 2], 1)

                def copy_max(key, turn, k):
                    bank, ps = full(key, turn)
                    wait(act, max_in, 16 * (BODY * turn + k - 1))
                    act.activation(max_rows[:, k % 2, :], ps[0:2 * HEADS, 0:128], ACT.Copy
                                   ).then_inc(w_free[bank], 1)

                def copy_pixels(key, turn, par, half):
                    bank, ps = full(key, turn)
                    act.activation(y_pix[:, par, 2 * half:2 * half + 2, :],
                                   ps[:, 0:2 * C].rearrange("p (r c) -> p r c", r=2), ACT.Copy
                                   ).then_inc(w_free[bank], 1)

                def normalise(group, par):
                    act.wait_ge(pix_ready, group + 1)
                    for r in range(QROWS):
                        act.activation(y_pix[:, par, r, :], y_pix[:, par, r, :], ACT.Identity,
                                       scale=pix_scale[:, par, 0, r:r + 1], bias=pix_scale[:, par, 1, r:r + 1]
                                       ).then_inc(pix_done, 1)

                def z_upper(key, turn, zpar, q, half):
                    bank, ps = full(key, turn)
                    src = by_window(ps)
                    for n in range(NCH):
                        last = act.activation(z_rows(z_hi, zpar, n, q, half), src(n), ACT.Copy)
                    last.then_inc(z_hi_done, 1)

                def qk_upper(key, turn, k, chunks):
                    v = BODY * turn + k
                    bank, ps = full(key, turn)
                    if chunks[0] == 0:
                        u = k - 2
                        wait(act, st_in[u % 3], 192 * (6 * turn + u // 3 + 1))
                    for i, c in enumerate(chunks):
                        last = act.activation(nat[:, k % 2, 0, c, :], ps[:, i * SEQ:(i + 1) * SEQ], ACT.Identity,
                                              bias=qk_bias[:, c:c + 1])
                    last.then_inc(qk_hi_done, 1)

                def reciprocals(turn, k):
                    v = BODY * turn + k
                    act.wait_ge(pv_done[0], v + 1)
                    act.wait_ge(pv_done[1], v + 1)
                    wait(act, o_ready, v)
                    act.activation(rinv[:], ps_r[0:CH, :], ACT.Ln).then_inc(ln_done, 1)
                    act.wait_ge(ln_done, v + 1)
                    act.activation(rinv[:], rinv[:], ACT.Exp, scale=-1.0).then_inc(rinv_ready, 1)

                for q in range(QROWS):
                    for half in range(2):
                        copy_pixels(("prep", q, f"turn{half}"), 0, q % 2, half)
                    normalise(q, q % 2)
                    for half in range(2):
                        z_upper(("prep", q, f"back{half}"), 0, 0, q, half)
                for k in (-3, -2, -1):
                    if k == -1:
                        copy_max((k, "max_rows"), 0, 0)
                    qk_upper((k, "qk01"), 0, k + 3, (0, 1))
                    qk_upper((k, "qk2"), 0, k + 3, (2,))

                with act.Fori(0, turns) as turn:
                    for k in range(BODY):
                        back, rows = groups_beside(k, BACK_AT), groups_beside(k, TURN_AT)
                        for h in range(HEADS):
                            if h == HEADS - 1 and back is not None:
                                group, par = next_group(turn, k, back)
                                normalise(group, par)
                            exponentials(turn, k, h)
                        copy_max((k, "max_rows"), turn, k + 1)
                        if back is not None:
                            for half in range(2):
                                z_upper((k, f"back{half}"), turn, (k // NWIN + 1) % 2, back, half)
                        reciprocals(turn, k)
                        qk_upper((k, "qk01"), turn, k + 3, (0, 1))
                        if rows is not None:
                            for half in range(2):
                                copy_pixels((k, f"turn{half}"), turn, rows % 2, half)
                        qk_upper((k, "qk2"), turn, k + 3, (2,))

            @block.vector
            def _(dve):
                def row_statistics(turn, group, m_count, xpar, q):
                    dve.wait_ge(x_in[xpar], m_count)
                    if not isinstance(group, int) or group >= 2:
                        dve.wait_ge(y_ready, group - 1)
                    for n in range(NCH):
                        for r in range(QROWS):
                            last = dve.bn_stats(row_stats[:, q % 2, n * QROWS + r, :],
                                                acc[:, xpar, n, (QROWS * q + r) * W:(QROWS * q + r + 1) * W])
                    last.then_inc(row_counts, 1)

                def pixel_statistics(keys, turn, par):
                    for key in keys:
                        bank, before = job(key, turn)
                        dve.wait_ge(w_free[bank], before + 1)
                    for r in range(QROWS):
                        last = dve.bn_stats(pix_stats[:, par, r, :], y_pix[:, par, r, :])
                    last.then_inc(pix_counts, 1)

                def z_lower(key, turn, zpar, group, q, half):
                    bank, _ = job(key, turn)
                    dve.wait_ge(z_hi_done, 2 * group + half + 1)
                    src = by_window(ps_w[bank])
                    for n in range(NCH):
                        last = dve.tensor_tensor(z_rows(z_lo, zpar, n, q, half), src(n),
                                                 z_rows(z_hi, zpar, n, q, half).bitcast(F32), ALU.subtract)
                    last.then_inc(w_free[bank], 1)

                def qk_lower(key, turn, k, chunks, nth):
                    v = BODY * turn + k
                    bank, _ = job(key, turn)
                    dve.wait_ge(qk_hi_done, 2 * v + nth + 1)
                    for i, c in enumerate(chunks):
                        last = dve.scalar_tensor_tensor(
                            out=nat[:, k % 2, 1, c, :], in0=ps_w[bank][:, i * SEQ:(i + 1) * SEQ],
                            scalar=qk_bias[:, c:c + 1], in1=nat[:, k % 2, 0, c, :].bitcast(F32),
                            op0=ALU.add, op1=ALU.subtract)
                    last.then_inc(w_free[bank], 1)

                def values(key, turn, k):
                    bank, before = job(key, turn)
                    dve.wait_ge(w_full[bank], before + 1)
                    wait(dve, pv_done[1], BODY * turn + k - 2)
                    dve.tensor_tensor(
                        v_sb[:, k % 3, :, :], ps_w[bank][:].rearrange("p (a c) -> p a c", a=2)[:, :, 0:C],
                        v_bias[:].unsqueeze(1).broadcast_to([128, 2, C]), ALU.add).then_inc(w_free[bank], 1)

                def maxima(turn, k, h):
                    v = BODY * turn + k
                    dve.wait_ge(s_full, HEADS * v + h + 1)
                    dve.tensor_reduce(neg_max[:, k % 2, 2 * h:2 * h + 2],
                                      ps_s[h % 2][:].rearrange("p (a t) -> p a t", a=2), AX.X, ALU.max,
                                      negate=True).then_inc(s_maxed[h % 2], 1)

                def output(turn, k):
                    v = BODY * turn + k
                    dve.wait_ge(rinv_ready, v + 1)
                    wait(dve, added[k % 2], 9 * turn + k // 2)
                    dve.tensor_tensor(o_sb[:, k % 2, :, :], ps_o[0:CH, :].rearrange("p (n s) -> p n s", n=NCH),
                                      rinv[:].rearrange("p (n s) -> p n s", n=NCH), ALU.mult).then_inc(o_ready, 1)

                for q in range(QROWS):
                    row_statistics(0, q, 16, 0, q)
                    pixel_statistics([("prep", q, f"turn{half}") for half in range(2)], 0, q % 2)
                    for half in range(2):
                        z_lower(("prep", q, f"back{half}"), 0, 0, q, q, half)
                for k in (-3, -2, -1):
                    if k == -1:
                        for h in range(HEADS):
                            maxima(0, 0, h)
                    qk_lower((k, "qk01"), 0, k + 3, (0, 1), 0)
                    qk_lower((k, "qk2"), 0, k + 3, (2,), 1)
                    values((k, "v"), 0, k + 3)

                with dve.Fori(0, turns) as turn:
                    for k in range(BODY):
                        first = groups_beside(k, ROW_AT)
                        back, rows = groups_beside(k, BACK_AT), groups_beside(k, TURN_AT)
                        for h in range(HEADS):
                            maxima(turn, k + 1, h)
                        if back is not None:
                            group, par = next_group(turn, k, back)
                            for half in range(2):
                                z_lower((k, f"back{half}"), turn, (k // NWIN + 1) % 2, group, back, half)
                        if first is not None:
                            group, par = next_group(turn, k, first)
                            m = k // NWIN + 1
                            row_statistics(turn, group, 16 * (turn + m // 2 + 1), m % 2, first)
                        output(turn, k)
                        qk_lower((k, "qk01"), turn, k + 3, (0, 1), 0)
                        if rows is not None:
                            pixel_statistics([(k, f"turn{half}") for half in range(2)], turn, rows % 2)
                        qk_lower((k, "qk2"), turn, k + 3, (2,), 1)
                        values((k, "v"), turn, k + 3)

            @block.sync
            def _(sp):
                def stack(turn, k):
                    v = BODY * turn + k
                    done = HEADS * (v - 2)
                    waits = []
                    for name in ("qk01", "qk2"):
                        bank, before = job((k - 3, name), turn)
                        waits.append((w_free[bank], before + 1))
                    if not isinstance(turn, int):
                        done, *counts = (sp.to_reg(c) for c in (done, *(c for _, c in waits)))
                        waits = [(s, c) for (s, _), c in zip(waits, counts)]
                    for s, c in waits:
                        sp.wait_ge(s, c)
                    wait(sp, t_full, done)
                    for part, lower_of in ((0, ()), (1, (0, 1)), (2, (2, 3))):
                        for blk in range(4):
                            lo = 1 if blk in lower_of else 0
                            sp.dma_start(st[k % 3][part * HD:(part + 1) * HD, 3 * blk:3 * blk + 3, :].bitcast(F32),
                                         nat[blk * HD:(blk + 1) * HD, k % 2, lo, :, :].bitcast(F32)
                                         ).then_inc(st_in[k % 3], 16)

                def max_row(turn, k):
                    bank, before = job((k - 1, "max_rows"), turn)
                    sp.wait_ge(w_free[bank], before + 1)
                    sp.dma_start(st[k % 3][CH:CH + 1, 0:HEADS, :].bitcast(F32).rearrange("p h (a n) -> p (h a) n", a=2),
                                 max_rows[:, k % 2, :].bitcast(F32)).then_inc(max_in, 16)

                stack(0, 0)
                stack(0, 1)
                max_row(0, 0)
                with sp.Fori(0, turns) as turn:
                    for k in range(BODY):
                        stack(turn, k + 2)
                        max_row(turn, k + 1)
                n = BODY * turns
                for i in range(3):
                    sp.wait_ge(st_in[i], 192 * len(range(i, n + 2, 3)))
                sp.wait_ge(max_in, 16 * (n + 1))

            @block.gpsimd
            def _(pool):
                ahead, count = QROWS * (RSTD_STEPS + 1 + RSTD_STEPS), [0, None]

                def done(ins):
                    ins.then_inc(pool_step, 1)
                    count[0] += 1

                def settle(stand_alone=False):
                    turn = count[1]
                    (wait_alone if stand_alone else wait)(
                        pool, pool_step, count[0] if turn is None else count[0] + STEPS_A_TURN * turn)

                def normalise_rows(group, q, xpar):
                    pool.wait_ge(row_counts, group + 1)
                    t = [row_tmp[:, i, :] for i in range(5)]
                    done(rstd(pool, done, settle, row_stats[:, q % 2, :, :], t[0:3], W, EPS_ROW, t[3], t[4],
                              minus_half[0:CH, 0:NCH * QROWS]))
                    settle(True)
                    for n in range(NCH):
                        for r in range(QROWS):
                            i = n * QROWS + r
                            last = pool.tensor_scalar(
                                y[:, q % 2, n, r, :], acc[:, xpar, n, (QROWS * q + r) * W:(QROWS * q + r + 1) * W],
                                t[3][:, i:i + 1], t[4][:, i:i + 1], ALU.mult, ALU.add)
                    last.then_inc(y_ready, 1)

                def pixel_scales(group, q):
                    pool.wait_ge(pix_counts, group + 1)
                    rstd(pool, done, settle, pix_stats[:, q % 2, :, :], [pix_tmp[:, i, :] for i in range(3)], C, EPS_PIX,
                         pix_scale[:, q % 2, 0, :], pix_scale[:, q % 2, 1, :],
                         minus_half[:, 0:QROWS]).then_inc(pix_ready, 1)

                def add_window(turn, k):
                    w, par = k % NWIN, k // NWIN
                    wait_alone(pool, o_ready, BODY * turn + k + 1)
                    o = o_sb[:, k % 2, :, :]
                    o_rows = o.rearrange("p n (r c) -> p (n r) c", c=WIN)
                    if w == 0:
                        edges = o_rows[:, :, STEP:WIN]
                    elif w == NWIN - 1:
                        edges = o_rows[:, :, 0:2]
                    else:
                        edges = bass.AP(tensor=o_rows.tensor, offset=o_rows.offset,
                                        ap=[list(o_rows.ap[0]), [WIN, NCH * WIN], [STEP, 2], [1, 2]])
                    done(pool.tensor_scalar(edges, edges, 0.5, 0.0, ALU.mult, ALU.add))
                    settle()
                    for e, part in enumerate((o[:, :, 0:EDGE], o[:, :, SEQ - EDGE:SEQ])):
                        done(pool.tensor_tensor(part, part, edge_weight[:, e, :].unsqueeze(1).broadcast_to(
                            [CH, NCH, EDGE]), ALU.mult))
                    settle()
                    a = acc[:, par, :, :].rearrange("p n (r c) -> p n r c", c=W)[:, :, :, STEP * w:STEP * w + WIN]
                    pool.tensor_tensor(a, a, o.rearrange("p n (r c) -> p n r c", c=WIN), ALU.add
                                       ).then_inc(added[k % 2], 1)
                    pool.wait_ge(added[k % 2], 9 * turn + k // 2 + 1)

                def edge_weights(turn, k):
                    i = (2 * turn + k // NWIN) % NWIN
                    top, bottom = (i + NWIN - 1) // NWIN, 1 - i // (NWIN - 1)
                    done(pool.tensor_copy(edge_weight[:, 0, :], one_half[:, bass.ds(top * EDGE, EDGE)]))
                    done(pool.tensor_copy(edge_weight[:, 1, :], one_half[:, bass.ds(bottom * EDGE, EDGE)]))
                    settle()

                def finish_band(turn, k):
                    par = k // NWIN
                    m = 2 * turn + par
                    b, i = m // NWIN, m % NWIN
                    at_end = i // (NWIN - 1)
                    flat = acc[:].rearrange("p a n s -> p (a n s)")
                    size, tail = NCH * WIN * W, 2 * W
                    here, there = par * size + STEP * W, (1 - par) * size
                    source = here + (there - here) * at_end
                    for n in range(NCH):
                        done(pool.tensor_copy(acc[:, 1 - par, n, 0:tail],
                                              flat[:, bass.ds(source + n * WIN * W, tail)]))
                    settle()
                    top = i * STEP * W
                    pool.dma_start(x2_v[b][:, :, bass.ds(top, STEP * W)], acc[:, par, :, 0:STEP * W]
                                   ).then_inc(stored[par], 16)
                    tail_image = B + (b - B) * at_end
                    pool.dma_start(x2_v[tail_image][:, :, bass.ds(top + STEP * W, tail)],
                                   acc[:, par, :, STEP * W:WIN * W]).then_inc(stored[par], 16)
                    pool.wait_ge(stored[par], 32 * (turn + 1))
                    m2 = (m + 2) % BANDS
                    pool.dma_start(acc[:, par, :, :],
                                   x_v[m2 // NWIN][:, :, bass.ds(m2 % NWIN * (STEP * W), WIN * W)]
                                   ).then_inc(x_in[par], 16)

                for m in range(2):
                    pool.dma_start(acc[:, m, :, :], x_v[0][:, :, m * STEP * W:(m * STEP + WIN) * W]
                                   ).then_inc(x_in[m], 16)
                for q in range(QROWS):
                    normalise_rows(q, q, 0)
                    pixel_scales(q, q)
                assert count[0] == ahead
                with pool.Fori(0, turns) as turn:
                    count[1] = turn
                    for k in range(BODY):
                        first, rows = groups_beside(k, ROW_AT), groups_beside(k, TURN_AT)
                        if k % NWIN == 0:
                            edge_weights(turn, k)
                        if first is not None:
                            group, par = next_group(turn, k, first)
                            normalise_rows(group, first, (k // NWIN + 1) % 2)
                        add_window(turn, k)
                        if rows is not None:
                            group, par = next_group(turn, k, rows)
                            pixel_scales(group, rows)
                        if k % NWIN == NWIN - 1:
                            finish_band(turn, k)
                    assert count[0] == ahead + STEPS_A_TURN
                for par in range(2):
                    pool.wait_ge(x_in[par], 16 * (turns + 1))


E, TOP = 8, 2
D = W
TOKENS = B * C * H
TILE = 128
TILES = 8
HALF = TILES // 2
BATCHES = TOKENS // (TILE * TILES)
RING = 4
MOE_TURNS = BATCHES // RING
EPS_TOKEN = 1e-5
ON_DVE = 4
SPLITS = 3

AUX_JOBS = ("turn0", "turn1", "logits0", "logits1", "by_token", "gates", "bias0", "bias1")
AUX = 4


GATE_STEPS = 9
MOE_STEPS_A_TURN = RING * (2 * TILES + RSTD_STEPS)


def experts(nc, x2, router_w, router_b, expert_w, expert_b, out, turns=MOE_TURNS):
    tok_in = x2.rearrange("b c h w -> (b c h) w").rearrange("(n p t) w -> n p (t w)", p=TILE, t=TILES)
    tok_out = out.rearrange("b c h w -> (b c h) w").rearrange("(n p t) w -> n p (t w)", p=TILE, t=TILES)

    with ExitStack() as ctx:
        def sb(name, shape, dt=F32):
            return ctx.enter_context(nc.sbuf_tensor(name, shape, dt))

        def sem(name):
            return ctx.enter_context(nc.semaphore(name))

        t_in = sb("t_in", [TILE, RING, TILES, D])
        t_norm = sb("t_norm", [TILE, 2, TILES, D])
        t_hi = sb("t_hi", [D, 2, TILES * TILE], F32R)
        t_lo = sb("t_lo", [D, 2, TILES * TILE], F32R)
        base = sb("base", [TILE, 2, TILES, D])
        part = sb("part", [TILE, 2, ON_DVE, D])
        scaled = sb("scaled", [TILE, 2, E - ON_DVE, D])
        t_out = sb("t_out", [TILE, 2, TILES, D])
        e_hi = sb("e_hi", [D, E, D], F32R)
        e_lo = sb("e_lo", [D, E, D], F32R)
        e_raw = sb("e_raw", [D, E, D])
        r_raw = sb("r_raw", [D, TILE])
        r_hi = sb("r_hi", [D, TILE], F32R)
        r_lo = sb("r_lo", [D, TILE], F32R)
        r_bias = sb("r_bias", [E, 1])
        stack = HALF * SPLITS * E
        b_raw = sb("b_raw", [stack, 2, HALF * D])
        b_cut = sb("b_cut", [stack, 2, HALF * D], F32R)
        b_stack = sb("b_stack", [stack, HALF * D], F32R)
        ident = sb("ident2", [128, 128])
        number = sb("number", [TILE, TILES, E])
        minus_half = sb("minus_half2", [TILE, TILES])
        counts = sb("counts", [TILE, 2, TILES, 6])
        stat_tmp = sb("stat_tmp", [TILE, 3, TILES])
        t_scale = sb("t_scale", [TILE, 2, 2, TILES])
        logits_t = sb("logits_t", [E, TILES * TILE])
        logits = sb("logits", [TILE, TILES, E])
        top = sb("top", [TILE, TILES, 8])
        top_at = sb("top_at", [TILE, TILES, 8], mybir.dt.uint32)
        top_no = sb("top_no", [TILE, TOP, TILES])
        gap = sb("gap", [TILE, 4, TILES])
        gate2 = sb("gate2", [TILE, TILES])
        chosen = sb("chosen", [TILE, TOP, TILES, E])
        gate = sb("gate", [TILE, 2, TILES, E])
        gate_cut = sb("gate_cut", [TILE, TILES, E], F32R)
        gate_parts = sb("gate_parts", [TILE, TILES, SPLITS, E])
        gate_t = sb("gate_t", [stack, 2, TILE], F32R)

        ps_y = [[ctx.enter_context(nc.psum_tensor(f"ps_y{i}{j}", [TILE, 512], F32)) for j in range(2)]
                for i in range(2)]
        ps_a = [ctx.enter_context(nc.psum_tensor(f"ps_a{i}", [128, 512], F32)) for i in range(AUX)]

        set_in, set_const, set_step = sem("set_in"), sem("set_const"), sem("set_step")
        with nc.Block() as block:
            @block.sync
            def _(sp):
                sp.wait_ge(set_const, 7)
                n = 0
                with nc.allow_non_contiguous_dma(reason="router weights, once"):
                    sp.dma_start(e_raw[:], expert_w.rearrange("e d c -> d e c")).then_inc(set_in, 16)
                    sp.dma_start(r_raw[:, 0:E], router_w).then_inc(set_in, 16)
                    sp.dma_start(r_bias[:], router_b.rearrange("(e a) -> e a", a=1)).then_inc(set_in, 16)
                    n += 3
                    for t in range(HALF):
                        for p in range(SPLITS):
                            r = (t * SPLITS + p) * E
                            sp.dma_start(b_raw[r:r + E, p // 2, t * D:(t + 1) * D], expert_b).then_inc(set_in, 16)
                            n += 1
                sp.wait_ge(set_in, 16 * n)

            @block.gpsimd
            def _(pool):
                pool.memset(ident[:], 0.0).then_inc(set_const, 1)
                pool.memset(r_raw[:], 0.0).then_inc(set_const, 1)
                pool.memset(minus_half[:], -0.5).then_inc(set_const, 1)
                pool.memset(b_raw[:, 0, :], 0.0).then_inc(set_const, 1)
                pool.memset(b_raw[:, 1, :], 0.0).then_inc(set_const, 1)
                pool.wait_ge(set_const, 5)
                pool.affine_select(out=ident[:], in_=ident[:], compare_op=ALU.not_equal, fill=1.0, base=0,
                                   pattern=[[-1, 128]], channel_multiplier=1).then_inc(set_const, 1)
                for e in range(E):
                    last = pool.memset(number[:, :, e:e + 1], float(e))
                last.then_inc(set_const, 1)

            @block.vector
            def _(dve):
                dve.wait_ge(set_in, 16 * (3 + HALF * SPLITS))
                dve.wait_ge(set_const, 7)
                dve.tensor_copy(e_hi[:], e_raw[:])
                dve.tensor_copy(r_hi[:], r_raw[:])
                dve.tensor_copy(b_cut[:], b_raw[:]).then_inc(set_step, 1)
                dve.wait_ge(set_step, 1)
                dve.tensor_tensor(e_lo[:], e_raw[:], e_hi[:].bitcast(F32), ALU.subtract)
                dve.tensor_tensor(r_lo[:], r_raw[:], r_hi[:].bitcast(F32), ALU.subtract)
                dve.tensor_tensor(b_raw[:, 1, :], b_raw[:, 1, :], b_cut[:, 1, :].bitcast(F32), ALU.subtract
                                  ).then_inc(set_step, 1)
                dve.wait_ge(set_step, 2)
                dve.tensor_tensor(b_stack[:], b_raw[:, 1, :], b_cut[:, 0, :].bitcast(F32), ALU.add)

        t_landed = [sem(f"t_landed{i}") for i in range(RING)]
        counted = sem("counted")
        scale_ready = sem("scale_ready")
        norm_done = sem("norm_done")
        hi_done = sem("hi_done")
        aux_full = [sem(f"aux_full{i}") for i in range(AUX)]
        aux_free = [sem(f"aux_free{i}") for i in range(AUX)]
        gap_ready = sem("gap_ready")
        gap_exp = sem("gap_exp")
        gates_ready = sem("gates_ready")
        y_full = sem("y_full")
        dve_read = [sem(f"dve_read{i}") for i in range(2)]
        act_read = [sem(f"act_read{i}") for i in range(2)]
        summed = [sem(f"summed{i}") for i in range(2)]
        moe_step = sem("moe_step")
        gate_step = sem("gate_step")
        sum_step = sem("sum_step")
        out_stored = [sem(f"out_stored{i}") for i in range(2)]

        def aux(turn, j, name):
            i = AUX_JOBS.index(name)
            return i % AUX, 2 * (RING * turn + j) + i // AUX

        def tiles_before(turn, j, t):
            return HALF * (RING * turn + j) + t // 2

        with nc.Block() as block:
            @block.sync
            def _(sp):
                def load(turn, j, address):
                    bank, before = aux(turn, j - RING, "bias1")
                    wait(sp, aux_free[bank], before + 1)
                    sp.dma_start(t_in[:, j % RING, :, :].rearrange("p t w -> p (t w)"), tok_in[address]
                                 ).then_inc(t_landed[j % RING], 16)

                for j in range(3):
                    load(0, j, j)
                with sp.Fori(0, turns) as turn:
                    for j in range(RING):
                        load(turn, j + 3, (RING * turn + j + 3) % BATCHES)
                        for q in range(2):
                            for i in range(2):
                                sp.wait_ge(summed[i], tiles_before(turn, j, HALF * (q + 1)))
                            sp.dma_start(tok_out[RING * turn + j][:, q * HALF * D:(q + 1) * HALF * D],
                                         t_out[:, j % 2, q * HALF:(q + 1) * HALF, :].rearrange("p t w -> p (t w)")
                                         ).then_inc(out_stored[j % 2], 16)
                for i in range(RING):
                    sp.wait_ge(t_landed[i], 16 * len(range(i, RING * turns + 3, RING)))
                for i in range(2):
                    sp.wait_ge(out_stored[i], 32 * 2 * turns)

            @block.tensor
            def _(pe):
                def take(turn, j, name):
                    bank, before = aux(turn, j, name)
                    wait(pe, aux_free[bank], before)
                    return bank, ps_a[bank]

                def turn_half(turn, j, half):
                    n = RING * turn + j
                    bank, ps = take(turn, j, f"turn{half}")
                    pe.wait_ge(norm_done, n + 1)
                    for t in range(HALF):
                        mm = pe.transpose(ps[:, t * TILE:(t + 1) * TILE], t_norm[:, j % 2, half * HALF + t, :], ident[:])
                    mm.then_inc(aux_full[bank], 1)

                def logits_half(turn, j, half):
                    turned, before = aux(turn, j, f"turn{half}")
                    pe.wait_ge(aux_free[turned], before + 1)
                    bank, ps = take(turn, j, f"logits{half}")
                    cols = slice(half * 512, (half + 1) * 512)
                    for i, (a, t) in enumerate(((r_hi, t_hi), (r_hi, t_lo), (r_lo, t_hi))):
                        mm = pe.matmul(ps[:], a[:], t[:, j % 2, cols], start=(i == 0), stop=(i == 2))
                    mm.then_inc(aux_full[bank], 1)

                def by_token(turn, j):
                    for half in range(2):
                        bank, before = aux(turn, j, f"logits{half}")
                        wait_alone(pe, aux_free[bank], before + 1)
                    bank, ps = take(turn, j, "by_token")
                    for t in range(TILES):
                        mm = pe.transpose(ps[:, t * E:(t + 1) * E], logits_t[:, t * TILE:(t + 1) * TILE],
                                          ident[0:E, 0:E])
                    mm.then_inc(aux_full[bank], 1)

                def turn_gates(turn, j):
                    bank, ps = take(turn, j, "gates")
                    pe.wait_ge(gates_ready, RING * turn + j + 1)
                    for half in range(2):
                        mm = pe.transpose(ps[0:stack, half * TILE:(half + 1) * TILE],
                                          gate_parts[:, half * HALF:(half + 1) * HALF, :, :].rearrange(
                                              "p t s e -> p (t s e)"), ident[:])
                    mm.then_inc(aux_full[bank], 1)

                def bias_half(turn, j, half):
                    if half == 0:
                        gates, before = aux(turn, j, "gates")
                        pe.wait_ge(aux_free[gates], before + 1)
                    bank, ps = take(turn, j, f"bias{half}")
                    pe.matmul(ps[:], gate_t[:, half, :], b_stack[:], start=True, stop=True).then_inc(aux_full[bank], 1)

                def expert_tile(turn, j, t):
                    wait(pe, dve_read[t % 2], tiles_before(turn, j, t))
                    wait(pe, act_read[t % 2], tiles_before(turn, j, t))
                    cols = slice(t * TILE, (t + 1) * TILE)
                    for tt, ws in ((t_hi, (e_hi, e_lo)), (t_lo, (e_hi,))):
                        for w in ws:
                            for b in range(2):
                                mm = pe.matmul(ps_y[t % 2][b][:], tt[:, j % 2, cols],
                                               w[:, 4 * b:4 * b + 4, :].rearrange("p e c -> p (e c)"),
                                               start=(tt is t_hi and w is e_hi), stop=(tt is t_lo))
                    mm.then_inc(y_full, 1)

                def job(turn, j, i):
                    name = AUX_JOBS[i]
                    if name.startswith("turn"):
                        turn_half(turn, j, i)
                    elif name.startswith("logits"):
                        logits_half(turn, j, i - 2)
                    elif name == "by_token":
                        by_token(turn, j)
                    elif name == "gates":
                        turn_gates(turn, j)
                    else:
                        bias_half(turn, j, i - 6)

                for i in range(TILES):
                    job(0, 0, i)
                with pe.Fori(0, turns) as turn:
                    for j in range(RING):
                        for t in range(TILES):
                            expert_tile(turn, j, t)
                            job(turn, j + 1, t)

            @block.scalar
            def _(act):
                act.preload_act_table_set("natural_log_exp_and_others")

                def full(turn, j, name):
                    bank, before = aux(turn, j, name)
                    act.wait_ge(aux_full[bank], before + 1)
                    return bank, ps_a[bank]

                def normalise(turn, j, tiles):
                    n = RING * turn + j
                    act.wait_ge(scale_ready, n + 1)
                    for t in tiles:
                        last = act.activation(t_norm[:, j % 2, t, :], t_in[:, j % RING, t, :], ACT.Identity,
                                              scale=t_scale[:, j % 2, 0, t:t + 1], bias=t_scale[:, j % 2, 1, t:t + 1])
                    if TILES - 1 in tiles:
                        last.then_inc(norm_done, 1)

                def job(turn, j, i):
                    name = AUX_JOBS[i]
                    n = RING * turn + j
                    if name.startswith("turn"):
                        bank, ps = full(turn, j, name)
                        act.activation(t_hi[:, j % 2, i * 512:(i + 1) * 512], ps[:], ACT.Copy).then_inc(hi_done, 1)
                    elif name.startswith("logits"):
                        bank, ps = full(turn, j, name)
                        act.activation(logits_t[:, (i - 2) * 512:(i - 1) * 512], ps[0:E, :], ACT.Identity,
                                       bias=r_bias[:]).then_inc(aux_free[bank], 1)
                    elif name == "by_token":
                        act.wait_ge(gap_ready, n + 1)
                        act.activation(gap[:, 1, :], gap[:, 0, :], ACT.Exp).then_inc(gap_exp, 1)
                    elif name == "gates":
                        bank, ps = full(turn, j, name)
                        act.activation(gate_t[:].rearrange("p h t -> p (h t)"), ps[0:stack, 0:2 * TILE], ACT.Copy
                                       ).then_inc(aux_free[bank], 1)

                def weigh(turn, j, t):
                    n = TILES * (RING * turn + j) + t
                    act.wait_ge(y_full, n + 1)
                    wait(act, summed[t % 2], tiles_before(turn, j, t))
                    for e in range(ON_DVE, E):
                        last = act.activation(scaled[:, t % 2, e - ON_DVE, :],
                                              ps_y[t % 2][1][:, (e - ON_DVE) * D:(e - ON_DVE + 1) * D], ACT.Copy,
                                              scale=gate[:, j % 2, t, e:e + 1])
                    last.then_inc(act_read[t % 2], 1)

                normalise(0, 0, range(TILES))
                for i in range(TILES):
                    job(0, 0, i)
                normalise(0, 1, range(TILES))
                with act.Fori(0, turns) as turn:
                    for j in range(RING):
                        for t in range(TILES):
                            weigh(turn, j, t)
                            job(turn, j + 1, t)
                            if t >= HALF:
                                normalise(turn, j + 2, range(2 * (t - HALF), 2 * (t - HALF) + 2))

            @block.vector
            def _(dve):
                def statistics(turn, j, tiles):
                    if 0 in tiles:
                        dve.wait_ge(t_landed[j % RING], 16 * (turn + j // RING + 1))
                    for t in tiles:
                        last = dve.bn_stats(counts[:, j % 2, t, :], t_in[:, j % RING, t, :])
                    if TILES - 1 in tiles:
                        last.then_inc(counted, 1)

                def choose(turn, j):
                    n = RING * turn + j
                    bank, before = aux(turn, j, "by_token")
                    dve.wait_ge(aux_full[bank], before + 1)
                    dve.tensor_copy(logits[:].rearrange("p t e -> p (t e)"), ps_a[bank][:, 0:TILES * E]
                                    ).then_inc(aux_free[bank], 1)
                    wait_alone(dve, aux_free[bank], before + 1)
                    step = GATE_STEPS * n
                    for t in range(TILES):
                        last = dve.max(top[:, t, :], logits[:, t, :])
                    last.then_inc(gate_step, 1)
                    dve.wait_ge(gate_step, step + 1)
                    dve.tensor_tensor(gap[:, 0, :], top[:, :, 1], top[:, :, 0], ALU.subtract).then_inc(gap_ready, 1)
                    for t in range(TILES):
                        last = dve.max_index(top_at[:, t, :], top[:, t, :], logits[:, t, :])
                    last.then_inc(gate_step, 1)
                    dve.wait_ge(gate_step, step + 2)
                    dve.tensor_copy(top_no[:], top_at[:, :, 0:TOP].rearrange("p t k -> p k t")).then_inc(gate_step, 1)
                    dve.wait_ge(gate_step, step + 3)
                    for k in range(TOP):
                        last = dve.tensor_tensor(chosen[:, k, :, :], number[:], wide(top_no[:, k, :]), ALU.is_equal)
                    dve.wait_ge(gap_exp, n + 1)
                    dve.tensor_scalar(gap[:, 2, :], gap[:, 1, :], 1.0, None, ALU.add).then_inc(gate_step, 1)
                    dve.wait_ge(gate_step, step + 4)
                    dve.reciprocal(gap[:, 3, :], gap[:, 2, :]).then_inc(gate_step, 1)
                    dve.wait_ge(gate_step, step + 5)
                    dve.tensor_tensor(gate2[:], gap[:, 1, :], gap[:, 3, :], ALU.mult)
                    dve.tensor_tensor(chosen[:, 0, :, :], chosen[:, 0, :, :], wide(gap[:, 3, :]), ALU.mult
                                      ).then_inc(gate_step, 1)
                    dve.wait_ge(gate_step, step + 6)
                    dve.tensor_tensor(chosen[:, 1, :, :], chosen[:, 1, :, :], wide(gate2[:]), ALU.mult
                                      ).then_inc(gate_step, 1)
                    dve.wait_ge(gate_step, step + 7)
                    dve.tensor_tensor(gate[:, j % 2, :, :], chosen[:, 0, :, :], chosen[:, 1, :, :], ALU.add
                                      ).then_inc(gate_step, 1)
                    dve.wait_ge(gate_step, step + 8)
                    dve.tensor_copy(gate_cut[:], gate[:, j % 2, :, :]).then_inc(gate_step, 1)
                    dve.wait_ge(gate_step, step + 9)
                    dve.tensor_copy(gate_parts[:, :, 0, :], gate_cut[:].bitcast(F32))
                    dve.tensor_copy(gate_parts[:, :, 2, :], gate_cut[:].bitcast(F32))
                    dve.tensor_tensor(gate_parts[:, :, 1, :], gate[:, j % 2, :, :], gate_cut[:].bitcast(F32),
                                      ALU.subtract).then_inc(gates_ready, 1)

                def wide(a):
                    return a.unsqueeze(2).broadcast_to([TILE, TILES, E])

                def job(turn, j, i):
                    name = AUX_JOBS[i]
                    n = RING * turn + j
                    bank, before = aux(turn, j, name)
                    if name.startswith("turn"):
                        dve.wait_ge(hi_done, 2 * n + i + 1)
                        cols = slice(i * 512, (i + 1) * 512)
                        dve.tensor_tensor(t_lo[:, j % 2, cols], ps_a[bank][:], t_hi[:, j % 2, cols].bitcast(F32),
                                          ALU.subtract).then_inc(aux_free[bank], 1)
                    elif name == "by_token":
                        choose(turn, j)
                    elif name.startswith("bias"):
                        half = i - 6
                        tiles = slice(half * HALF, (half + 1) * HALF)
                        dve.wait_ge(aux_full[bank], before + 1)
                        dve.tensor_tensor(base[:, j % 2, tiles, :], ps_a[bank][:].rearrange("p (t c) -> p t c", t=HALF),
                                          t_in[:, j % RING, tiles, :], ALU.add).then_inc(aux_free[bank], 1)

                def weigh(turn, j, t):
                    n = TILES * (RING * turn + j) + t
                    dve.wait_ge(y_full, n + 1)
                    wait(dve, summed[t % 2], tiles_before(turn, j, t))
                    before = base[:, j % 2, t, :]
                    if t in (0, HALF):
                        bank, done = aux(turn, j, f"bias{t // HALF}")
                        dve.wait_ge(aux_free[bank], done + 1)
                    for e in range(ON_DVE):
                        ins = dve.scalar_tensor_tensor(
                            out=part[:, t % 2, e, :], in0=ps_y[t % 2][0][:, e * D:(e + 1) * D],
                            scalar=gate[:, j % 2, t, e:e + 1], in1=before, op0=ALU.mult, op1=ALU.add)
                        before = part[:, t % 2, e, :]
                        if e < ON_DVE - 1:
                            ins.then_inc(sum_step, 1)
                            dve.wait_ge(sum_step, (ON_DVE - 1) * n + e + 1)
                        else:
                            ins.then_inc(dve_read[t % 2], 1)

                statistics(0, 0, range(TILES))
                statistics(0, 1, range(TILES))
                for i in range(TILES):
                    job(0, 0, i)
                with dve.Fori(0, turns) as turn:
                    for j in range(RING):
                        for t in range(TILES):
                            weigh(turn, j, t)
                            job(turn, j + 1, t)
                            if t < HALF:
                                statistics(turn, j + 2, range(2 * t, 2 * t + 2))

            @block.gpsimd
            def _(pool):
                count = [0, None]

                def done(ins):
                    ins.then_inc(moe_step, 1)
                    count[0] += 1

                def settle(stand_alone=False):
                    turn = count[1]
                    (wait_alone if stand_alone else wait)(
                        pool, moe_step, count[0] if turn is None else count[0] + MOE_STEPS_A_TURN * turn)

                def scales(turn, j):
                    pool.wait_ge(counted, RING * turn + j + 1)
                    wait(pool, scale_ready, RING * turn + j)
                    rstd(pool, done, settle, counts[:, j % 2, :, :], [stat_tmp[:, i, :] for i in range(3)], D, EPS_TOKEN,
                         t_scale[:, j % 2, 0, :], t_scale[:, j % 2, 1, :], minus_half[:]).then_inc(scale_ready, 1)

                def add_up(turn, j, t):
                    s = scaled[:, t % 2, :, :]
                    pool.wait_ge(act_read[t % 2], tiles_before(turn, j, t) + 1)
                    done(pool.tensor_tensor(s[:, 0:2, :], s[:, 0:2, :], s[:, 2:4, :], ALU.add))
                    settle()
                    done(pool.tensor_tensor(s[:, 0, :], s[:, 0, :], s[:, 1, :], ALU.add))
                    settle()
                    pool.wait_ge(dve_read[t % 2], tiles_before(turn, j, t) + 1)
                    if t == 0:
                        wait(pool, out_stored[j % 2], 32 * (2 * turn + j // 2))
                    pool.tensor_tensor(t_out[:, j % 2, t, :], s[:, 0, :], part[:, t % 2, ON_DVE - 1, :], ALU.add
                                       ).then_inc(summed[t % 2], 1)

                scales(0, 0)
                scales(0, 1)
                ahead = count[0]
                with pool.Fori(0, turns) as turn:
                    count[1] = turn
                    for j in range(RING):
                        for t in range(TILES):
                            add_up(turn, j, t)
                            if t == HALF - 1:
                                scales(turn, j + 2)
                    assert count[0] == ahead + MOE_STEPS_A_TURN


_INS = ['x', 'L0_conv_Wq', 'L0_conv_Wk', 'L0_conv_Wv', 'L0_conv_ln_gamma', 'L0_conv_ln_beta',
        'L0_ffn_router_w', 'L0_ffn_router_b', 'L0_ffn_expert_w', 'L0_ffn_expert_b']
_OUT = (B, C, H, W)


def metaformer(nc, x, wq, wk, wv, gamma, beta, router_w, router_b, expert_w, expert_b, out):
    mixed = nc.dram_tensor("mixed", (B + 1, C, H, W), F32).ap()
    attention(nc, x, wq, wk, wv, gamma, beta, mixed)
    experts(nc, mixed, router_w, router_b, expert_w, expert_b, out)


def kernel(**inputs):
    import numpy as _np
    import concourse.bacc as _bacc
    from concourse import mybir as _mybir
    from concourse.bass_utils import run_bass_kernel_spmd as _run

    nc = _bacc.Bacc("TRN2", target_bir_lowering=False, num_devices=1)
    arrays, args = {}, []
    for name in _INS:
        a = _np.ascontiguousarray(inputs[name])
        arrays[f"in_{name}_dram"] = a
        args.append(nc.dram_tensor(f"in_{name}_dram", a.shape, _mybir.dt.from_np(a.dtype), kind="ExternalInput").ap())
    args.append(nc.dram_tensor("out_0_dram", _OUT, _mybir.dt.float32, kind="ExternalOutput").ap())
    metaformer(nc, *args)
    r = _run(nc, [arrays], core_ids=[0])
    return r.results[0]["out_0_dram"]
```

```python
from contextlib import ExitStack

import concourse.bass as bass
from concourse import mybir

F32 = mybir.dt.float32
F32R = mybir.dt.float32r
ACT = mybir.ActivationFunctionType
ALU = mybir.AluOpType
AX = mybir.AxisListType

B, C, H, W = 4, 192, 128, 128
HEADS = 6
HD = C // HEADS
CH = 96
NCH = C // CH
HC = CH // HD
WIN, STEP = 16, 14
NWIN = (H - WIN) // STEP + 1
BANDS = B * NWIN
SEQ = WIN * WIN
BODY = 2 * NWIN
TURNS = BANDS // 2
QROWS = 4
SCALE = float(C) ** -0.5
EPS_ROW, EPS_PIX = 1e-6, 1e-5

STATS_AT, TURN_AT, BACK_AT = 0, 1, 2

JOBS = ("qk01", "max_rows", "turn0", "turn1", "qk2", "v", "back0", "back1")

RSTD_STEPS = 9
EDGE = 2 * WIN
STEPS_A_TURN = 2 * (QROWS * 2 * RSTD_STEPS + 3 * NWIN + 2 + NCH)


PREP = (("turn", 0), ("turn", 1), ("back", 0), ("turn", 2), ("back", 1), ("turn", 3), ("back", 2), ("back", 3))


def groups_beside(k, first):
    q = k % NWIN - first
    return q if 0 <= q < QROWS else None


def jobs_beside(k):
    out = []
    for name in JOBS:
        if name.startswith("back") and groups_beside(k, BACK_AT) is None:
            continue
        if name.startswith("turn") and groups_beside(k, TURN_AT) is None:
            continue
        out.append(name)
    return out


def job_table():
    table, n = {}, 0
    for what, q in PREP:
        for half in range(2):
            table[("prep", q, f"{what}{half}")] = n
            n += 1
    for k, names in ((-3, ("qk01", "qk2")), (-2, ("qk01", "qk2", "v")), (-1, ("qk01", "max_rows", "qk2", "v"))):
        for name in names:
            table[(k, name)] = n
            n += 1
    ahead = n
    for k in range(BODY):
        for name in jobs_beside(k):
            table[(k, name)] = n
            n += 1
    assert (n - ahead) % 2 == 0
    return table, (n - ahead) // 2


JOB, JOBS_A_TURN = job_table()


def wait(engine, sem, value):
    if isinstance(value, int) and value <= 0:
        return
    engine.wait_ge(sem, value)


def wait_alone(engine, sem, value):
    if not isinstance(value, int):
        value = engine.to_reg(value)
        engine.wait_ge(sem, 1)
    engine.wait_ge(sem, value)


def variances(pool, done, settle, stats, tmp, count, eps):
    total, diff, spread = tmp
    done(pool.tensor_tensor(total, stats[:, :, 1], stats[:, :, 4], ALU.add))
    done(pool.tensor_tensor(diff, stats[:, :, 1], stats[:, :, 4], ALU.subtract))
    done(pool.tensor_tensor(spread, stats[:, :, 2], stats[:, :, 5], ALU.add))
    settle()
    done(pool.tensor_tensor(diff, diff, diff, ALU.mult))
    done(pool.tensor_scalar(spread, spread, 4.0 / count, 0.0, ALU.mult, ALU.add))
    settle()
    done(pool.tensor_tensor(diff, diff, spread, ALU.add))
    settle(True)
    done(pool.tensor_scalar(diff, diff, 0.25, eps, ALU.mult, ALU.add))


def rstd(pool, done, settle, tmp, scale_out, shift_out, minus_half):
    total, diff, spread = tmp
    settle()
    done(pool.tensor_tensor(scale_out, diff, minus_half, ALU.pow))
    settle()
    done(pool.tensor_tensor(spread, total, scale_out, ALU.mult))
    settle(True)
    return pool.tensor_scalar(shift_out, spread, -0.5, 0.0, ALU.mult, ALU.add)


def attention(nc, x, wq, wk, wv, gamma, beta, x2, turns=TURNS):
    x_v = x.rearrange("b (n c) h w -> b c n (h w)", n=NCH)
    x2_v = x2.rearrange("b (n c) h w -> b c n (h w)", n=NCH)

    with ExitStack() as ctx:
        def sb(name, shape, dt=F32):
            return ctx.enter_context(nc.sbuf_tensor(name, shape, dt))

        def sem(name):
            return ctx.enter_context(nc.semaphore(name))

        acc = sb("acc", [CH, 2, NCH, WIN * W])
        y = sb("y", [CH, 2, NCH, QROWS, W])
        y_pix = sb("y_pix", [W, 2, QROWS, C])
        z_hi = sb("z_hi", [CH, 2, NCH, NWIN, SEQ], F32R)
        z_lo = sb("z_lo", [CH, 2, NCH, NWIN, SEQ], F32R)
        nat = sb("nat", [128, 2, 2, 3, SEQ], F32R)
        st = [sb(f"st{i}", [CH + 1, 2 * HEADS, SEQ], F32R) for i in range(3)]
        v_sb = sb("v_sb", [128, 3, 2, C])
        prob = sb("prob", [128, HEADS, 2 * SEQ])
        rinv = sb("rinv", [CH, NCH * SEQ])
        o_sb = sb("o_sb", [CH, 2, NCH, SEQ])
        neg_max = sb("neg_max", [128, 2, 2 * HEADS])
        max_rows = sb("max_rows", [2 * HEADS, 2, 128], F32R)
        row_stats = sb("row_stats", [CH, 2, NCH * QROWS, 6])
        row_tmp = sb("row_tmp", [CH, 6, NCH * QROWS])
        pix_stats = sb("pix_stats", [W, 2, QROWS, 6])
        pix_tmp = sb("pix_tmp", [W, 4, QROWS])
        pix_scale = sb("pix_scale", [W, 2, 2, QROWS])
        minus_half = sb("minus_half", [128, NCH * QROWS])
        wqk_hi = sb("wqk_hi", [CH, NCH, 3 * 128], F32R)
        wqk_lo = sb("wqk_lo", [CH, NCH, 3 * 128], F32R)
        wv_hi = sb("wv_hi", [CH, NCH, SEQ], F32R)
        wv_lo = sb("wv_lo", [CH, NCH, SEQ], F32R)
        qk_bias = sb("qk_bias", [128, 3])
        v_bias = sb("v_bias", [128, C])
        ident = sb("ident", [128, 128])
        ones = sb("ones", [128, HD])
        one_half = sb("one_half", [CH, 2 * EDGE])
        edge_weight = sb("edge_weight", [CH, 2, EDGE])
        gb = sb("gb", [CH, 2, NCH])

        ps_s = [ctx.enter_context(nc.psum_tensor(f"ps_s{i}", [128, 512], F32)) for i in range(2)]
        ps_t = [ctx.enter_context(nc.psum_tensor(f"ps_t{i}", [128, 512], F32)) for i in range(2)]
        ps_w = [ctx.enter_context(nc.psum_tensor(f"ps_w{i}", [128, 512], F32)) for i in range(2)]
        ps_o = ctx.enter_context(nc.psum_tensor("ps_o", [128, 512], F32))
        ps_r = ctx.enter_context(nc.psum_tensor("ps_r", [128, 512], F32))

        sums_aside = [ps_r[CH:128, 0:SEQ], ps_r[CH:128, SEQ:2 * SEQ], ps_o[CH:128, 0:SEQ]]

        raw = prob[0:CH, :, :].rearrange("p a b -> p (a b)")
        w_raw = raw[:, 0:3 * NCH * C].rearrange("p (t n c) -> p t n c", t=3, n=NCH)
        w_t = raw[:, 3 * NCH * C:6 * NCH * C].rearrange("p (t n q) -> p t n q", t=3, n=NCH)
        w_slot = raw[:, 6 * NCH * C:6 * NCH * C + NCH * 384].rearrange("p (n q) -> p n q", n=NCH)
        scaled = y[:, 0, :, :, :].rearrange("p n r w -> p (n r w)")[:, 0:NCH * 384].rearrange(
            "p (n q) -> p n q", n=NCH)
        scaled_v = y[:, 1, :, :, :].rearrange("p n r w -> p (n r w)")[:, 0:NCH * C].rearrange(
            "p (n q) -> p n q", n=NCH)
        beta_wide = o_sb[:, 0, :, 0:128]

        w_in = sem("w_in")
        const = sem("const")
        w_turned = sem("w_turned")
        w_copied = sem("w_copied")
        w_step = sem("w_step")
        bias_ready = sem("bias_ready")

        with nc.Block() as block:
            @block.sync
            def _(sp):
                for t, w in enumerate((wq, wk, wv)):
                    sp.dma_start(w_raw[:, t, :, :], w.rearrange("(n p) c -> p n c", n=NCH)).then_inc(w_in, 16)
                for t, w in enumerate((gamma, beta)):
                    for n in range(NCH):
                        sp.dma_start(gb[:, t, n:n + 1], w[n * CH:(n + 1) * CH].rearrange("(p a) -> p a", a=1)
                                     ).then_inc(w_in, 16)

            @block.gpsimd
            def _(pool):
                pool.memset(ident[:], 0.0).then_inc(const, 1)
                pool.memset(ones[:], 1.0).then_inc(const, 1)
                pool.memset(minus_half[:], -0.5).then_inc(const, 1)
                pool.memset(one_half[:, 0:EDGE], 1.0).then_inc(const, 1)
                pool.memset(one_half[:, EDGE:], 0.5).then_inc(const, 1)
                pool.memset(wv_hi[:].bitcast(F32), 0.0).then_inc(const, 1)
                pool.memset(wv_lo[:].bitcast(F32), 0.0).then_inc(const, 1)
                pool.wait_ge(const, 7)
                pool.affine_select(out=ident[:], in_=ident[:], compare_op=ALU.not_equal, fill=1.0, base=0,
                                   pattern=[[-1, 128]], channel_multiplier=1).then_inc(const, 1)

            @block.tensor
            def _(pe):
                pe.wait_ge(const, 8)
                pe.wait_ge(w_in, 16 * (3 + 2 * NCH))
                for t, bank in enumerate((ps_s[0], ps_s[1], ps_t[0])):
                    for n in range(NCH):
                        for qn in range(NCH):
                            last = pe.transpose(bank[0:CH, n * C + qn * CH:n * C + (qn + 1) * CH],
                                                w_raw[:, t, qn, n * CH:(n + 1) * CH], ident[0:CH, 0:CH])
                    last.then_inc(w_turned, 1)
                pe.wait_ge(w_step, 3)
                for c in range(3):
                    for n in range(NCH):
                        pe.matmul(ps_t[1][:, c:c + 1], w_slot[:, n, c * 128:(c + 1) * 128], gb[:, 1, n:n + 1],
                                  start=(n == 0), stop=(n == NCH - 1))
                for n in range(NCH):
                    last = pe.matmul(ps_w[0][:, 0:C], beta_wide[:, n, :], w_t[:, 2, n, :],
                                     start=(n == 0), stop=(n == NCH - 1))
                last.then_inc(bias_ready, 1)

            @block.vector
            def _(dve):
                for slot in st:
                    dve.memset(slot[CH:CH + 1, :, :].bitcast(F32), 1.0)
                for t, bank in enumerate((ps_s[0], ps_s[1], ps_t[0])):
                    dve.wait_ge(w_turned, t + 1)
                    dve.tensor_copy(w_t[:, t, :, :], bank[0:CH, 0:NCH * C].rearrange("p (n q) -> p n q", n=NCH)
                                    ).then_inc(w_copied, 1)
                dve.wait_ge(w_copied, 3)
                for t in range(2):
                    for n in range(NCH):
                        last = dve.tensor_copy(
                            w_slot[:, n, :].rearrange("p (c b d) -> p b c d", c=3, b=4)[:, 2 * t:2 * t + 2],
                            w_t[:, t, n, :].rearrange("p (b c d) -> p b c d", b=2, c=3))
                last.then_inc(w_step, 1)
                dve.tensor_copy(beta_wide, gb[:, 1, :].unsqueeze(2).broadcast_to([CH, NCH, 128])
                                ).then_inc(w_step, 1)
                dve.wait_ge(w_step, 2)
                for n in range(NCH):
                    dve.tensor_scalar(scaled[:, n, :], w_slot[:, n, :], gb[:, 0, n:n + 1], None, ALU.mult)
                    last = dve.tensor_scalar(scaled_v[:, n, :], w_t[:, 2, n, :], gb[:, 0, n:n + 1], None, ALU.mult)
                last.then_inc(w_step, 1)
                dve.wait_ge(w_step, 3)
                dve.wait_ge(const, 8)
                dve.tensor_copy(wqk_hi[:], scaled)
                dve.tensor_copy(wv_hi[:, :, 0:C], scaled_v).then_inc(w_step, 1)
                dve.wait_ge(w_step, 4)
                dve.tensor_tensor(wqk_lo[:], scaled, wqk_hi[:].bitcast(F32), ALU.subtract)
                dve.tensor_tensor(wv_lo[:, :, 0:C], scaled_v, wv_hi[:, :, 0:C].bitcast(F32), ALU.subtract)
                dve.wait_ge(bias_ready, 1)
                dve.tensor_copy(qk_bias[:], ps_t[1][:, 0:3])
                dve.tensor_copy(v_bias[:], ps_w[0][:, 0:C]).then_inc(w_step, 1)

        x_in = [sem(f"x_in{p}") for p in range(2)]
        row_counts = sem("row_counts")
        y_in = [sem(f"y_in{i}") for i in range(2)]
        row_ready = sem("row_ready")
        y_low = sem("y_low")
        y_high = sem("y_high")
        pix_counts = sem("pix_counts")
        pix_ready = sem("pix_ready")
        pix_done = sem("pix_done")
        z_hi_done = sem("z_hi_done")
        qk_hi_done = sem("qk_hi_done")
        w_full = [sem(f"w_full{i}") for i in range(2)]
        w_free = [sem(f"w_free{i}") for i in range(2)]
        st_in = [sem(f"st_in{i}") for i in range(3)]
        s_full = sem("s_full")
        s_maxed = [sem(f"s_maxed{i}") for i in range(2)]
        max_in = sem("max_in")
        t_full = sem("t_full")
        exp_done = [sem(f"exp_done{i}") for i in range(2)]
        pv_done = [sem(f"pv_done{i}") for i in range(2)]
        ln_done = sem("ln_done")
        rinv_ready = sem("rinv_ready")
        o_ready = sem("o_ready")
        added = [sem(f"added{i}") for i in range(2)]
        pool_step = sem("pool_step")
        stored = [sem(f"stored{p}") for p in range(2)]

        def job(key, turn):
            n = JOB[key]
            return n % 2, n // 2 if key[0] == "prep" else n // 2 + turn * JOBS_A_TURN

        def pe_steps(pe):
            def scores(turn, k, h):
                v = BODY * turn + k
                slot = st[k % 3]
                if h == 0:
                    wait(pe, st_in[k % 3], 192 * (6 * turn + k // 3 + 1))
                wait(pe, s_maxed[h % 2], 3 * v + h // 2)
                for half in range(2):
                    mm = pe.matmul(ps_s[h % 2][:, half * SEQ:(half + 1) * SEQ],
                                   slot[0:CH, h, half * 128:(half + 1) * 128], slot[0:CH, HEADS + h, :],
                                   start=True, stop=True)
                mm.then_inc(s_full, 1)

            def scores_t(turn, k, h):
                v = BODY * turn + k
                slot = st[k % 3]
                if h == 0:
                    pe.wait_ge(max_in, 16 * (v + 1))
                wait(pe, exp_done[h % 2], 3 * v + h // 2)
                for half in range(2):
                    mm = pe.matmul(ps_t[h % 2][:, half * SEQ:(half + 1) * SEQ],
                                   slot[:, HEADS + h, half * 128:(half + 1) * 128], slot[:, h, :],
                                   start=True, stop=True)
                mm.then_inc(t_full, 1)

            def weigh(turn, k, n, half):
                v = BODY * turn + k
                heads = range(HC * n, HC * (n + 1))
                if half == 0:
                    for h in heads:
                        wait(pe, exp_done[h % 2], 3 * v + h // 2 + 1)
                    if n == 0:
                        wait(pe, o_ready, v)
                        wait(pe, ln_done, v)
                for a, h in enumerate(heads):
                    mm = pe.matmul(ps_o[a * HD:(a + 1) * HD, n * SEQ:(n + 1) * SEQ],
                                   v_sb[:, k % 3, half, h * HD:(h + 1) * HD], prob[:, h, half * SEQ:(half + 1) * SEQ],
                                   start=(half == 0), stop=(half == 1), tile_position=(0, a * HD))
                if n == 0:
                    mm = sum_aside(0, half)
                else:
                    sum_aside(1 + half, 0)
                    for a, h in enumerate(heads):
                        pe.matmul(ps_r[a * HD:(a + 1) * HD, SEQ:2 * SEQ], ones[:],
                                  prob[:, h, half * SEQ:(half + 1) * SEQ],
                                  start=(half == 0), stop=(half == 1), tile_position=(0, a * HD))
                    mm = sum_aside(1 + half, 1)
                if half == 1:
                    mm.then_inc(pv_done[n], 1)

            def sum_aside(h, half):
                return pe.matmul(sums_aside[h], ones[:], prob[:, h, half * SEQ:(half + 1) * SEQ],
                                 start=(half == 0), stop=(half == 1), tile_position=(0, HC * HD))

            def take(key, turn):
                bank, before = job(key, turn)
                wait(pe, w_free[bank], before)
                return bank, ps_w[bank]

            def max_turn(key, turn, k):
                v = BODY * turn + k
                bank, ps = take(key, turn)
                for i in range(2):
                    pe.wait_ge(s_maxed[i], 3 * (v + 1))
                pe.transpose(ps[0:2 * HEADS, 0:128], neg_max[:, k % 2, :], ident[:]).then_inc(w_full[bank], 1)

            def turn_rows(key, turn, group, par, half):
                bank, ps = take(key, turn)
                if half == 0:
                    pe.wait_ge(y_low, group + 1)
                    pe.wait_ge(y_high, group + 1)
                for r in range(2):
                    for n in range(NCH):
                        mm = pe.transpose(ps[:, r * C + n * CH:r * C + (n + 1) * CH],
                                          y[:, par, n, 2 * half + r, :], ident[0:CH, 0:CH])
                mm.then_inc(w_full[bank], 1)

            def turn_back(key, turn, group, par, half):
                bank, ps = take(key, turn)
                pe.wait_ge(pix_done, QROWS * group + 2 * half + 2)
                for n in range(NCH):
                    for r in range(2):
                        mm = pe.transpose(ps[0:CH, (2 * n + r) * W:(2 * n + r + 1) * W],
                                          y_pix[:, par, 2 * half + r, n * CH:(n + 1) * CH], ident[:])
                mm.then_inc(w_full[bank], 1)

            def project(key, turn, k, chunks, part=None):
                par, w = k // NWIN % 2, k % NWIN
                bank = job(key, turn)[0] if part == 1 else take(key, turn)[0]
                ps = ps_w[bank]
                for i, c in enumerate(chunks):
                    if part not in (None, i):
                        continue
                    parts = [(a, z, n) for a, z in ((wqk_hi, z_hi), (wqk_hi, z_lo), (wqk_lo, z_hi))
                             for n in range(NCH)]
                    for j, (a, z, n) in enumerate(parts):
                        mm = pe.matmul(ps[:, i * SEQ:(i + 1) * SEQ], a[:, n, c * 128:(c + 1) * 128],
                                       z[:, par, n, w, :], start=(j == 0), stop=(j == len(parts) - 1))
                if part != 0:
                    mm.then_inc(w_full[bank], 1)

            def project_v(key, turn, k):
                par, w = k // NWIN % 2, k % NWIN
                bank, ps = take(key, turn)
                for half in range(2):
                    parts = [(a, z, n) for a, z in ((wv_hi, z_hi), (wv_hi, z_lo), (wv_lo, z_hi))
                             for n in range(NCH)]
                    for j, (a, z, n) in enumerate(parts):
                        mm = pe.matmul(ps[:, half * SEQ:(half + 1) * SEQ],
                                       z[:, par, n, w, half * 128:(half + 1) * 128], a[:, n, :],
                                       start=(j == 0), stop=(j == len(parts) - 1))
                mm.then_inc(w_full[bank], 1)

            return scores, scores_t, weigh, max_turn, turn_rows, turn_back, project, project_v

        def by_window(ps):
            def of(n):
                t = ps[0:CH, 2 * n * W:(2 * n + 2) * W].rearrange("p (r w) -> p r w", r=2)
                return overlapped(t)
            return of

        def overlapped(t):
            part, row = list(t.ap[0]), list(t.ap[1])
            return bass.AP(tensor=t.tensor, offset=t.offset, ap=[part, [STEP, NWIN], row, [1, WIN]])

        def z_rows(z, zpar, n, q, half):
            r = QROWS * q + 2 * half
            return z[:, zpar, n, :, r * WIN:(r + 2) * WIN].rearrange("p v (r c) -> p v r c", r=2)

        def next_group(turn, k, q):
            return 2 * QROWS * turn + QROWS * (k // NWIN + 1) + q, q % 2

        with nc.Block() as block:
            @block.tensor
            def _(pe):
                (scores, scores_t, weigh, max_turn, turn_rows, turn_back, project, project_v) = pe_steps(pe)

                def z_complete(key, turn):
                    bank, before = job(key, turn)
                    pe.wait_ge(w_free[bank], before + 1)

                for what, q in PREP:
                    for half in range(2):
                        step = turn_rows if what == "turn" else turn_back
                        step(("prep", q, f"{what}{half}"), 0, q, q % 2, half)
                z_complete(("prep", QROWS - 1, "back1"), 0)
                for k in (-3, -2, -1):
                    if k == -1:
                        for h in range(HEADS):
                            scores(0, 0, h)
                    project((k, "qk01"), 0, k + 3, (0, 1))
                    if k == -1:
                        max_turn((k, "max_rows"), 0, 0)
                    project((k, "qk2"), 0, k + 3, (2,))
                    if k > -3:
                        project_v((k, "v"), 0, k + 2)
                for h in range(2):
                    scores_t(0, 0, h)
                    scores(0, 1, h)
                scores_t(0, 0, 2)
                scores(0, 1, 2)
                scores(0, 1, 3)

                with pe.Fori(0, turns) as turn:
                    for k in range(BODY):
                        back, rows = groups_beside(k, BACK_AT), groups_beside(k, TURN_AT)
                        if k % NWIN == NWIN - 3:
                            z_complete((k - 1, "back1"), turn)
                        project((k, "qk01"), turn, k + 3, (0, 1), 0)
                        scores(turn, k + 1, HEADS - 2)
                        project((k, "qk01"), turn, k + 3, (0, 1), 1)
                        scores(turn, k + 1, HEADS - 1)
                        scores_t(turn, k, HEADS - 3)
                        scores_t(turn, k, HEADS - 2)
                        weigh(turn, k, 0, 0)
                        max_turn((k, "max_rows"), turn, k + 1)
                        weigh(turn, k, 0, 1)
                        if rows is not None:
                            group, par = next_group(turn, k, rows)
                            for half in range(2):
                                turn_rows((k, f"turn{half}"), turn, group, par, half)
                        scores_t(turn, k, HEADS - 1)
                        project((k, "qk2"), turn, k + 3, (2,))
                        project_v((k, "v"), turn, k + 2)
                        weigh(turn, k, 1, 0)
                        if back is not None:
                            group, par = next_group(turn, k, back)
                            turn_back((k, "back0"), turn, group, par, 0)
                        scores(turn, k + 2, 0)
                        if back is not None:
                            turn_back((k, "back1"), turn, group, par, 1)
                        scores(turn, k + 2, 1)
                        scores_t(turn, k + 1, 0)
                        weigh(turn, k, 1, 1)
                        scores_t(turn, k + 1, 1)
                        scores(turn, k + 2, 2)
                        scores_t(turn, k + 1, 2)
                        scores(turn, k + 2, 3)

            @block.scalar
            def _(act):
                act.preload_act_table_set("natural_log_exp_and_others")

                def full(key, turn):
                    bank, before = job(key, turn)
                    act.wait_ge(w_full[bank], before + 1)
                    return bank, ps_w[bank]

                def exponentials(turn, k, h):
                    v = BODY * turn + k
                    act.wait_ge(t_full, HEADS * v + h + 1)
                    wait(act, pv_done[min(h, 1)], v)
                    act.activation(prob[:, h, :], ps_t[h % 2][:], ACT.Exp, scale=SCALE
                                   ).then_inc(exp_done[h % 2], 1)

                def copy_max(key, turn, k):
                    bank, ps = full(key, turn)
                    wait(act, max_in, 16 * (BODY * turn + k - 1))
                    act.activation(max_rows[:, k % 2, :], ps[0:2 * HEADS, 0:128], ACT.Copy
                                   ).then_inc(w_free[bank], 1)

                def copy_pixels(key, turn, par, half):
                    bank, ps = full(key, turn)
                    act.activation(y_pix[:, par, 2 * half:2 * half + 2, :],
                                   ps[:, 0:2 * C].rearrange("p (r c) -> p r c", r=2), ACT.Copy
                                   ).then_inc(w_free[bank], 1)

                def y_rows(group, par):
                    act.wait_ge(row_ready, group + 1)
                    for r in range(QROWS):
                        last = act.activation(y[:, par, 0, r, :], y[:, par, 0, r, :], ACT.Identity,
                                              scale=row_tmp[:, 3, r:r + 1], bias=row_tmp[:, 4, r:r + 1])
                    last.then_inc(y_low, 1)

                def normalise(group, par, half):
                    act.wait_ge(pix_ready, group + 1)
                    for r in range(2 * half, 2 * half + 2):
                        act.activation(y_pix[:, par, r, :], y_pix[:, par, r, :], ACT.Identity,
                                       scale=pix_scale[:, par, 0, r:r + 1], bias=pix_scale[:, par, 1, r:r + 1]
                                       ).then_inc(pix_done, 1)

                def z_upper(key, turn, zpar, q, half):
                    bank, ps = full(key, turn)
                    src = by_window(ps)
                    for n in range(NCH):
                        last = act.activation(z_rows(z_hi, zpar, n, q, half), src(n), ACT.Copy)
                    last.then_inc(z_hi_done, 1)

                def qk_upper(key, turn, k, chunks):
                    bank, ps = full(key, turn)
                    if chunks[0] == 0:
                        u = k - 2
                        wait(act, st_in[u % 3], 192 * (6 * turn + u // 3 + 1))
                    for i, c in enumerate(chunks):
                        last = act.activation(nat[:, k % 2, 0, c, :], ps[:, i * SEQ:(i + 1) * SEQ], ACT.Identity,
                                              bias=qk_bias[:, c:c + 1])
                    last.then_inc(qk_hi_done, 1)

                def reciprocals(turn, k):
                    v = BODY * turn + k
                    act.wait_ge(pv_done[0], v + 1)
                    act.wait_ge(pv_done[1], v + 1)
                    wait(act, o_ready, v)
                    for h in range(HC):
                        act.activation(rinv[h * HD:(h + 1) * HD, 0:SEQ], sums_aside[h], ACT.Ln)
                    act.activation(rinv[:, SEQ:2 * SEQ], ps_r[0:CH, SEQ:2 * SEQ], ACT.Ln).then_inc(ln_done, 1)
                    act.wait_ge(ln_done, v + 1)
                    act.activation(rinv[:], rinv[:], ACT.Exp, scale=-1.0).then_inc(rinv_ready, 1)

                for what, q in PREP:
                    if what == "turn":
                        y_rows(q, q % 2)
                        for half in range(2):
                            copy_pixels(("prep", q, f"turn{half}"), 0, q % 2, half)
                    else:
                        for half in range(2):
                            normalise(q, q % 2, half)
                        for half in range(2):
                            z_upper(("prep", q, f"back{half}"), 0, 0, q, half)
                for k in (-3, -2, -1):
                    qk_upper((k, "qk01"), 0, k + 3, (0, 1))
                    if k == -1:
                        copy_max((k, "max_rows"), 0, 0)
                    qk_upper((k, "qk2"), 0, k + 3, (2,))
                for h in range(HEADS - 3):
                    exponentials(0, 0, h)

                with act.Fori(0, turns) as turn:
                    for k in range(BODY):
                        back, rows = groups_beside(k, BACK_AT), groups_beside(k, TURN_AT)
                        qk_upper((k, "qk01"), turn, k + 3, (0, 1))
                        if rows == 0:
                            y_rows(*next_group(turn, k, rows))
                        exponentials(turn, k, HEADS - 3)
                        exponentials(turn, k, HEADS - 2)
                        copy_max((k, "max_rows"), turn, k + 1)
                        if back is not None:
                            normalise(*next_group(turn, k, back), 0)
                        if rows is not None:
                            for half in range(2):
                                copy_pixels((k, f"turn{half}"), turn, rows % 2, half)
                        exponentials(turn, k, HEADS - 1)
                        if back is not None:
                            normalise(*next_group(turn, k, back), 1)
                        qk_upper((k, "qk2"), turn, k + 3, (2,))
                        if back is not None:
                            for half in range(2):
                                z_upper((k, f"back{half}"), turn, (k // NWIN + 1) % 2, back, half)
                        exponentials(turn, k + 1, 0)
                        reciprocals(turn, k)
                        coming = groups_beside(k + 1, TURN_AT)
                        if coming not in (None, 0):
                            y_rows(*next_group(turn, k + 1, coming))
                        exponentials(turn, k + 1, 1)
                        exponentials(turn, k + 1, 2)

            @block.vector
            def _(dve):
                def row_statistics(turn, group, q):
                    dve.wait_ge(y_in[q % 2], 8 * (group + 2 - q % 2))
                    if not isinstance(group, int) or group >= 2:
                        dve.wait_ge(row_ready, group - 1)
                    for n in range(NCH):
                        for r in range(QROWS):
                            last = dve.bn_stats(row_stats[:, q % 2, n * QROWS + r, :], y[:, q % 2, n, r, :])
                    last.then_inc(row_counts, 1)

                def y_rows(group, par):
                    dve.wait_ge(row_ready, group + 1)
                    for r in range(QROWS):
                        i = QROWS + r
                        last = dve.tensor_scalar(y[:, par, 1, r, :], y[:, par, 1, r, :], row_tmp[:, 3, i:i + 1],
                                                 row_tmp[:, 4, i:i + 1], ALU.mult, ALU.add)
                    last.then_inc(y_high, 1)

                def pixel_statistics(keys, turn, par):
                    for key in keys:
                        bank, before = job(key, turn)
                        dve.wait_ge(w_free[bank], before + 1)
                    for r in range(QROWS):
                        last = dve.bn_stats(pix_stats[:, par, r, :], y_pix[:, par, r, :])
                    last.then_inc(pix_counts, 1)

                def z_lower(key, turn, zpar, group, q, half):
                    bank, _ = job(key, turn)
                    dve.wait_ge(z_hi_done, 2 * group + half + 1)
                    src = by_window(ps_w[bank])
                    for n in range(NCH):
                        last = dve.tensor_tensor(z_rows(z_lo, zpar, n, q, half), src(n),
                                                 z_rows(z_hi, zpar, n, q, half).bitcast(F32), ALU.subtract)
                    last.then_inc(w_free[bank], 1)

                def qk_lower(key, turn, k, chunks, nth):
                    v = BODY * turn + k
                    bank, _ = job(key, turn)
                    dve.wait_ge(qk_hi_done, 2 * v + nth + 1)
                    for i, c in enumerate(chunks):
                        last = dve.scalar_tensor_tensor(
                            out=nat[:, k % 2, 1, c, :], in0=ps_w[bank][:, i * SEQ:(i + 1) * SEQ],
                            scalar=qk_bias[:, c:c + 1], in1=nat[:, k % 2, 0, c, :].bitcast(F32),
                            op0=ALU.add, op1=ALU.subtract)
                    last.then_inc(w_free[bank], 1)

                def values(key, turn, k):
                    bank, before = job(key, turn)
                    dve.wait_ge(w_full[bank], before + 1)
                    wait(dve, pv_done[1], BODY * turn + k - 2)
                    dve.tensor_tensor(
                        v_sb[:, k % 3, :, :], ps_w[bank][:].rearrange("p (a c) -> p a c", a=2)[:, :, 0:C],
                        v_bias[:].unsqueeze(1).broadcast_to([128, 2, C]), ALU.add).then_inc(w_free[bank], 1)

                def maxima(turn, k, h):
                    v = BODY * turn + k
                    dve.wait_ge(s_full, HEADS * v + h + 1)
                    dve.tensor_reduce(neg_max[:, k % 2, 2 * h:2 * h + 2],
                                      ps_s[h % 2][:].rearrange("p (a t) -> p a t", a=2), AX.X, ALU.max,
                                      negate=True).then_inc(s_maxed[h % 2], 1)

                def output(turn, k):
                    v = BODY * turn + k
                    dve.wait_ge(rinv_ready, v + 1)
                    wait(dve, added[k % 2], 9 * turn + k // 2)
                    dve.tensor_tensor(o_sb[:, k % 2, :, :], ps_o[0:CH, :].rearrange("p (n s) -> p n s", n=NCH),
                                      rinv[:].rearrange("p (n s) -> p n s", n=NCH), ALU.mult).then_inc(o_ready, 1)

                row_statistics(0, 0, 0)
                row_statistics(0, 1, 1)
                for what, q in PREP:
                    if what == "turn":
                        y_rows(q, q % 2)
                        pixel_statistics([("prep", q, f"turn{half}") for half in range(2)], 0, q % 2)
                    else:
                        for half in range(2):
                            z_lower(("prep", q, f"back{half}"), 0, 0, q, q, half)
                        if q + 2 < QROWS:
                            row_statistics(0, q + 2, q)
                for k in (-3, -2, -1):
                    if k == -1:
                        for h in range(HEADS):
                            maxima(0, 0, h)
                    qk_lower((k, "qk01"), 0, k + 3, (0, 1), 0)
                    qk_lower((k, "qk2"), 0, k + 3, (2,), 1)
                    if k > -3:
                        values((k, "v"), 0, k + 2)
                for h in range(HEADS - 2):
                    maxima(0, 1, h)

                with dve.Fori(0, turns) as turn:
                    for k in range(BODY):
                        first = groups_beside(k, STATS_AT)
                        back, rows = groups_beside(k, BACK_AT), groups_beside(k, TURN_AT)
                        maxima(turn, k + 1, HEADS - 2)
                        if rows is not None:
                            y_rows(*next_group(turn, k, rows))
                        maxima(turn, k + 1, HEADS - 1)
                        qk_lower((k, "qk01"), turn, k + 3, (0, 1), 0)
                        if first is not None:
                            row_statistics(turn, next_group(turn, k, first)[0], first)
                        if rows is not None:
                            pixel_statistics([(k, f"turn{half}") for half in range(2)], turn, rows % 2)
                        qk_lower((k, "qk2"), turn, k + 3, (2,), 1)
                        values((k, "v"), turn, k + 2)
                        maxima(turn, k + 2, 0)
                        if back is not None:
                            group, _ = next_group(turn, k, back)
                            z_lower((k, "back0"), turn, (k // NWIN + 1) % 2, group, back, 0)
                        maxima(turn, k + 2, 1)
                        if back is not None:
                            z_lower((k, "back1"), turn, (k // NWIN + 1) % 2, group, back, 1)
                        maxima(turn, k + 2, 2)
                        maxima(turn, k + 2, 3)
                        output(turn, k)
                row_statistics(0, QROWS * (2 * turns + 1), 0)

            @block.sync
            def _(sp):
                def stack(turn, k):
                    v = BODY * turn + k
                    done = HEADS * (v - 2)
                    waits = []
                    for name in ("qk01", "qk2"):
                        bank, before = job((k - 3, name), turn)
                        waits.append((w_free[bank], before + 1))
                    if not isinstance(turn, int):
                        done, *counts = (sp.to_reg(c) for c in (done, *(c for _, c in waits)))
                        waits = [(s, c) for (s, _), c in zip(waits, counts)]
                    for s, c in waits:
                        sp.wait_ge(s, c)
                    wait(sp, t_full, done)
                    for part, lower_of in ((0, ()), (1, (0, 1)), (2, (2, 3))):
                        for blk in range(4):
                            lo = 1 if blk in lower_of else 0
                            sp.dma_start(st[k % 3][part * HD:(part + 1) * HD, 3 * blk:3 * blk + 3, :].bitcast(F32),
                                         nat[blk * HD:(blk + 1) * HD, k % 2, lo, :, :].bitcast(F32)
                                         ).then_inc(st_in[k % 3], 16)

                def max_row(turn, k):
                    bank, before = job((k - 1, "max_rows"), turn)
                    sp.wait_ge(w_free[bank], before + 1)
                    sp.dma_start(st[k % 3][CH:CH + 1, 0:HEADS, :].bitcast(F32).rearrange("p h (a n) -> p (h a) n", a=2),
                                 max_rows[:, k % 2, :].bitcast(F32)).then_inc(max_in, 16)

                def load_rows(turn, band, q):
                    group = 2 * QROWS * turn + QROWS * band + q
                    if not isinstance(group, int) or group >= 2:
                        sp.wait_ge(pix_counts, group - 1)
                    m = (2 * turn + band) % BANDS
                    sp.dma_start(y[:, q % 2, :, :, :].rearrange("p n r w -> p n (r w)"),
                                 x_v[m // NWIN][:, :, bass.ds(m % NWIN * (STEP * W) + q * QROWS * W, QROWS * W)]
                                 ).then_inc(y_in[q % 2], 16)

                for q in range(QROWS):
                    load_rows(0, 0, q)
                load_rows(0, 1, 0)
                stack(0, 0)
                stack(0, 1)
                max_row(0, 0)
                with sp.Fori(0, turns) as turn:
                    for k in range(BODY):
                        stack(turn, k + 2)
                        max_row(turn, k + 1)
                        if (k + 1) % NWIN < QROWS:
                            load_rows(turn, (k + 1) // NWIN + 1, (k + 1) % NWIN)
                n = BODY * turns
                for i in range(3):
                    sp.wait_ge(st_in[i], 192 * len(range(i, n + 2, 3)))
                sp.wait_ge(max_in, 16 * (n + 1))
                groups = QROWS * (2 * turns + 1) + 1
                for i in range(2):
                    sp.wait_ge(y_in[i], 16 * len(range(i, groups, 2)))

            @block.gpsimd
            def _(pool):
                ahead, count = (QROWS * 2 + 1) * RSTD_STEPS, [0, None]

                def done(ins):
                    ins.then_inc(pool_step, 1)
                    count[0] += 1

                def settle(stand_alone=False):
                    turn = count[1]
                    (wait_alone if stand_alone else wait)(
                        pool, pool_step, count[0] if turn is None else count[0] + STEPS_A_TURN * turn)

                def row_scales(group, q):
                    pool.wait_ge(row_counts, group + 1)
                    wait(pool, y_low, group)
                    wait(pool, y_high, group)
                    t = [row_tmp[:, i, :] for i in range(5)]
                    variances(pool, done, settle, row_stats[:, q % 2, :, :], t[0:3], W, EPS_ROW)
                    rstd(pool, done, settle, t[0:3], t[3], t[4], minus_half[0:CH, 0:NCH * QROWS]
                         ).then_inc(row_ready, 1)

                def pixel_scales(group, q):
                    pool.wait_ge(pix_counts, group + 1)
                    wait(pool, pix_ready, group)
                    t = [pix_tmp[:, i, :] for i in range(3)]
                    variances(pool, done, settle, pix_stats[:, q % 2, :, :], t, C, EPS_PIX)
                    rstd(pool, done, settle, t, pix_scale[:, q % 2, 0, :], pix_scale[:, q % 2, 1, :],
                         minus_half[:, 0:QROWS]).then_inc(pix_ready, 1)

                def add_window(turn, k):
                    w, par = k % NWIN, k // NWIN
                    wait_alone(pool, o_ready, BODY * turn + k + 1)
                    o = o_sb[:, k % 2, :, :]
                    o_rows = o.rearrange("p n (r c) -> p (n r) c", c=WIN)
                    if w == 0:
                        edges = o_rows[:, :, STEP:WIN]
                    elif w == NWIN - 1:
                        edges = o_rows[:, :, 0:2]
                    else:
                        edges = bass.AP(tensor=o_rows.tensor, offset=o_rows.offset,
                                        ap=[list(o_rows.ap[0]), [WIN, NCH * WIN], [STEP, 2], [1, 2]])
                    done(pool.tensor_scalar(edges, edges, 0.5, 0.0, ALU.mult, ALU.add))
                    settle()
                    for e, part in enumerate((o[:, :, 0:EDGE], o[:, :, SEQ - EDGE:SEQ])):
                        done(pool.tensor_tensor(part, part, edge_weight[:, e, :].unsqueeze(1).broadcast_to(
                            [CH, NCH, EDGE]), ALU.mult))
                    settle()
                    a = acc[:, par, :, :].rearrange("p n (r c) -> p n r c", c=W)[:, :, :, STEP * w:STEP * w + WIN]
                    pool.tensor_tensor(a, a, o.rearrange("p n (r c) -> p n r c", c=WIN), ALU.add
                                       ).then_inc(added[k % 2], 1)
                    pool.wait_ge(added[k % 2], 9 * turn + k // 2 + 1)

                def edge_weights(turn, k):
                    i = (2 * turn + k // NWIN) % NWIN
                    top, bottom = (i + NWIN - 1) // NWIN, 1 - i // (NWIN - 1)
                    done(pool.tensor_copy(edge_weight[:, 0, :], one_half[:, bass.ds(top * EDGE, EDGE)]))
                    done(pool.tensor_copy(edge_weight[:, 1, :], one_half[:, bass.ds(bottom * EDGE, EDGE)]))
                    settle()

                def finish_band(turn, k):
                    par = k // NWIN
                    m = 2 * turn + par
                    b, i = m // NWIN, m % NWIN
                    pool.wait_ge(x_in[1 - par], 16 * (turn + par + 1))
                    at_end = i // (NWIN - 1)
                    flat = acc[:].rearrange("p a n s -> p (a n s)")
                    size, tail = NCH * WIN * W, 2 * W
                    here, there = par * size + STEP * W, (1 - par) * size
                    source = here + (there - here) * at_end
                    for n in range(NCH):
                        done(pool.tensor_copy(acc[:, 1 - par, n, 0:tail],
                                              flat[:, bass.ds(source + n * WIN * W, tail)]))
                    settle()
                    top = i * STEP * W
                    pool.dma_start(x2_v[b][:, :, bass.ds(top, STEP * W)], acc[:, par, :, 0:STEP * W]
                                   ).then_inc(stored[par], 16)
                    tail_image = B + (b - B) * at_end
                    pool.dma_start(x2_v[tail_image][:, :, bass.ds(top + STEP * W, tail)],
                                   acc[:, par, :, STEP * W:WIN * W]).then_inc(stored[par], 16)

                def next_rows(turn, par):
                    wait(pool, stored[par], 32 * (turn + 1 - par))
                    m = (2 * turn + 2 - par) % BANDS
                    pool.dma_start(acc[:, par, :, :],
                                   x_v[m // NWIN][:, :, bass.ds(m % NWIN * (STEP * W), WIN * W)]
                                   ).then_inc(x_in[par], 16)

                pool.dma_start(acc[:, 0, :, :], x_v[0][:, :, 0:WIN * W]).then_inc(x_in[0], 16)
                row_scales(0, 0)
                for q in range(QROWS):
                    if q % 2 == 0:
                        row_scales(q + 1, q + 1)
                    pixel_scales(q, q)
                    if q == 1:
                        row_scales(2, 2)
                pool.wait_ge(x_in[0], 16)
                row_scales(QROWS, 0)
                assert count[0] == ahead
                with pool.Fori(0, turns) as turn:
                    count[1] = turn
                    for k in range(BODY):
                        first, rows = groups_beside(k, STATS_AT), groups_beside(k, TURN_AT)
                        if k % NWIN == 0:
                            edge_weights(turn, k)
                        if first not in (None, 0):
                            row_scales(next_group(turn, k, first)[0], first)
                        if rows is not None:
                            pixel_scales(next_group(turn, k, rows)[0], rows)
                        add_window(turn, k)
                        if k % NWIN == 1:
                            next_rows(turn, 1 - k // NWIN)
                        if k % NWIN == NWIN - 1:
                            row_scales(next_group(turn, k + 1, 0)[0], 0)
                            finish_band(turn, k)
                    assert count[0] == ahead + STEPS_A_TURN
                for par in range(2):
                    pool.wait_ge(stored[par], 32 * turns)


E, TOP = 8, 2
D = W
TOKENS = B * C * H
TILE = 128
TILES = 8
HALF = TILES // 2
BATCHES = TOKENS // (TILE * TILES)
RING = 6
MOE_TURNS = BATCHES // RING
EPS_TOKEN = 1e-5
ON_DVE = 4
SPLITS = 3

AUX_JOBS = ("turn0", "turn1", "logits0", "logits1", "by_token", "gates", "bias0", "bias1")
AUX_AT = (0, 0, 2, 2, 3, 6, 7, 7)
AUX = 2
YBANKS = 3
SUMS = 4
CHOOSE_AT, CHOOSE_STEPS = 3, 12
SCALES_AT = 1
STATS_AHEAD = 6
NORM_AT = 5


GATE_STEPS = 9
MOE_STEPS_A_TURN = RING * (2 * TILES + RSTD_STEPS)


def experts(nc, x2, router_w, router_b, expert_w, expert_b, out, turns=MOE_TURNS):
    tok_in = x2.rearrange("b c h w -> (b c h) w").rearrange("(n p t) w -> n p (t w)", p=TILE, t=TILES)
    tok_out = out.rearrange("b c h w -> (b c h) w").rearrange("(n p t) w -> n p (t w)", p=TILE, t=TILES)

    with ExitStack() as ctx:
        def sb(name, shape, dt=F32):
            return ctx.enter_context(nc.sbuf_tensor(name, shape, dt))

        def sem(name):
            return ctx.enter_context(nc.semaphore(name))

        t_in = sb("t_in", [TILE, RING, TILES, D])
        t_norm = sb("t_norm", [TILE, 2, TILES, D])
        t_hi = sb("t_hi", [D, 2, TILES * TILE], F32R)
        t_lo = sb("t_lo", [D, 2, TILES * TILE], F32R)
        base = sb("base", [TILE, 2, TILES, D])
        part = sb("part", [TILE, SUMS, ON_DVE, D])
        scaled = sb("scaled", [TILE, SUMS, E - ON_DVE, D])
        t_out = sb("t_out", [TILE, 2, TILES, D])
        e_hi = sb("e_hi", [D, E, D], F32R)
        e_lo = sb("e_lo", [D, E, D], F32R)
        e_raw = sb("e_raw", [D, E, D])
        r_raw = sb("r_raw", [D, TILE])
        r_hi = sb("r_hi", [D, TILE], F32R)
        r_lo = sb("r_lo", [D, TILE], F32R)
        r_bias = sb("r_bias", [E, 1])
        stack = HALF * SPLITS * E
        b_raw = sb("b_raw", [stack, 2, HALF * D])
        b_cut = sb("b_cut", [stack, 2, HALF * D], F32R)
        b_stack = sb("b_stack", [stack, HALF * D], F32R)
        ident = sb("ident2", [128, 128])
        number = sb("number", [TILE, TILES, E])
        minus_half = sb("minus_half2", [TILE, TILES])
        counts = sb("counts", [TILE, 2, TILES, 6])
        stat_tmp = sb("stat_tmp", [TILE, 3, TILES])
        t_scale = sb("t_scale", [TILE, 2, 2, TILES])
        logits_t = sb("logits_t", [E, TILES * TILE])
        logits = sb("logits", [TILE, TILES, E])
        top = sb("top", [TILE, TILES, 8])
        top_at = sb("top_at", [TILE, TILES, 8], mybir.dt.uint32)
        top_no = sb("top_no", [TILE, TOP, TILES])
        gap = sb("gap", [TILE, 4, TILES])
        gate2 = sb("gate2", [TILE, TILES])
        chosen = sb("chosen", [TILE, TOP, TILES, E])
        gate = sb("gate", [TILE, 2, TILES, E])
        gate_cut = sb("gate_cut", [TILE, TILES, E], F32R)
        gate_parts = sb("gate_parts", [TILE, TILES, SPLITS, E])
        gate_t = sb("gate_t", [stack, 2, TILE], F32R)

        ps_y = [[ctx.enter_context(nc.psum_tensor(f"ps_y{i}{j}", [TILE, 512], F32)) for j in range(2)]
                for i in range(YBANKS)]
        ps_a = [ctx.enter_context(nc.psum_tensor(f"ps_a{i}", [128, 512], F32)) for i in range(AUX)]

        set_in, set_const, set_step = sem("set_in"), sem("set_const"), sem("set_step")
        with nc.Block() as block:
            @block.sync
            def _(sp):
                sp.wait_ge(set_const, 7)
                n = 0
                with nc.allow_non_contiguous_dma(reason="router weights, once"):
                    sp.dma_start(e_raw[:], expert_w.rearrange("e d c -> d e c")).then_inc(set_in, 16)
                    sp.dma_start(r_raw[:, 0:E], router_w).then_inc(set_in, 16)
                    sp.dma_start(r_bias[:], router_b.rearrange("(e a) -> e a", a=1)).then_inc(set_in, 16)
                    n += 3
                    for t in range(HALF):
                        for p in range(SPLITS):
                            r = (t * SPLITS + p) * E
                            sp.dma_start(b_raw[r:r + E, p // 2, t * D:(t + 1) * D], expert_b).then_inc(set_in, 16)
                            n += 1
                sp.wait_ge(set_in, 16 * n)

            @block.gpsimd
            def _(pool):
                pool.memset(ident[:], 0.0).then_inc(set_const, 1)
                pool.memset(r_raw[:], 0.0).then_inc(set_const, 1)
                pool.memset(minus_half[:], -0.5).then_inc(set_const, 1)
                pool.memset(b_raw[:, 0, :], 0.0).then_inc(set_const, 1)
                pool.memset(b_raw[:, 1, :], 0.0).then_inc(set_const, 1)
                pool.wait_ge(set_const, 5)
                pool.affine_select(out=ident[:], in_=ident[:], compare_op=ALU.not_equal, fill=1.0, base=0,
                                   pattern=[[-1, 128]], channel_multiplier=1).then_inc(set_const, 1)
                for e in range(E):
                    last = pool.memset(number[:, :, e:e + 1], float(e))
                last.then_inc(set_const, 1)

            @block.vector
            def _(dve):
                dve.wait_ge(set_in, 16 * (3 + HALF * SPLITS))
                dve.wait_ge(set_const, 7)
                dve.tensor_copy(e_hi[:], e_raw[:])
                dve.tensor_copy(r_hi[:], r_raw[:])
                dve.tensor_copy(b_cut[:], b_raw[:]).then_inc(set_step, 1)
                dve.wait_ge(set_step, 1)
                dve.tensor_tensor(e_lo[:], e_raw[:], e_hi[:].bitcast(F32), ALU.subtract)
                dve.tensor_tensor(r_lo[:], r_raw[:], r_hi[:].bitcast(F32), ALU.subtract)
                dve.tensor_tensor(b_raw[:, 1, :], b_raw[:, 1, :], b_cut[:, 1, :].bitcast(F32), ALU.subtract
                                  ).then_inc(set_step, 1)
                dve.wait_ge(set_step, 2)
                dve.tensor_tensor(b_stack[:], b_raw[:, 1, :], b_cut[:, 0, :].bitcast(F32), ALU.add)

        t_landed = [sem(f"t_landed{i}") for i in range(RING)]
        counted = sem("counted")
        scale_ready = sem("scale_ready")
        norm_done = sem("norm_done")
        hi_done = sem("hi_done")
        aux_full = [sem(f"aux_full{i}") for i in range(AUX)]
        aux_free = [sem(f"aux_free{i}") for i in range(AUX)]
        gap_ready = sem("gap_ready")
        gap_exp = sem("gap_exp")
        gates_ready = sem("gates_ready")
        y_full = sem("y_full")
        dve_read = [sem(f"dve_read{i}") for i in range(YBANKS)]
        act_read = [sem(f"act_read{i}") for i in range(YBANKS)]
        summed = [sem(f"summed{i}") for i in range(SUMS)]
        moe_step = sem("moe_step")
        gate_step = sem("gate_step")
        sum_step = sem("sum_step")
        out_stored = [sem(f"out_stored{i}") for i in range(2)]

        def aux(turn, j, name):
            i = AUX_JOBS.index(name)
            return i % AUX, len(AUX_JOBS) // AUX * (RING * turn + j) + i // AUX

        def jobs_at(t):
            return [i for i, at in enumerate(AUX_AT) if at == t]

        def y_bank(turn, j, t):
            n = TILES * j + t
            return n % YBANKS, TILES * RING // YBANKS * turn + n // YBANKS

        def sums_before(turn, j, t):
            return TILES // SUMS * (RING * turn + j) + t // SUMS

        with nc.Block() as block:
            @block.sync
            def _(sp):
                def load(turn, j, address):
                    bank, before = aux(turn, j - 4, "bias1")
                    wait(sp, aux_free[bank], before + 1)
                    sp.dma_start(t_in[:, j % RING, :, :].rearrange("p t w -> p (t w)"), tok_in[address]
                                 ).then_inc(t_landed[j % RING], 16)

                for j in range(3):
                    load(0, j, j)
                with sp.Fori(0, turns) as turn:
                    for j in range(RING):
                        load(turn, j + 3, (RING * turn + j + 3) % BATCHES)
                        for q in range(2):
                            for i in range(SUMS):
                                sp.wait_ge(summed[i], sums_before(turn, j, HALF * (q + 1) + i))
                            sp.dma_start(tok_out[RING * turn + j][:, q * HALF * D:(q + 1) * HALF * D],
                                         t_out[:, j % 2, q * HALF:(q + 1) * HALF, :].rearrange("p t w -> p (t w)")
                                         ).then_inc(out_stored[j % 2], 16)
                for i in range(RING):
                    sp.wait_ge(t_landed[i], 16 * len(range(i, RING * turns + 3, RING)))
                for i in range(2):
                    sp.wait_ge(out_stored[i], 32 * (RING // 2) * turns)

            @block.tensor
            def _(pe):
                def take(turn, j, name):
                    bank, before = aux(turn, j, name)
                    wait(pe, aux_free[bank], before)
                    return bank, ps_a[bank]

                def turn_half(turn, j, half):
                    n = RING * turn + j
                    bank, ps = take(turn, j, f"turn{half}")
                    pe.wait_ge(norm_done, n + 1)
                    for t in range(HALF):
                        mm = pe.transpose(ps[:, t * TILE:(t + 1) * TILE], t_norm[:, j % 2, half * HALF + t, :], ident[:])
                    mm.then_inc(aux_full[bank], 1)

                def logits_half(turn, j, half):
                    turned, before = aux(turn, j, f"turn{half}")
                    pe.wait_ge(aux_free[turned], before + 1)
                    bank, ps = take(turn, j, f"logits{half}")
                    cols = slice(half * 512, (half + 1) * 512)
                    for i, (a, t) in enumerate(((r_hi, t_hi), (r_hi, t_lo), (r_lo, t_hi))):
                        mm = pe.matmul(ps[:], a[:], t[:, j % 2, cols], start=(i == 0), stop=(i == 2))
                    mm.then_inc(aux_full[bank], 1)

                def by_token(turn, j):
                    for half in range(2):
                        bank, before = aux(turn, j, f"logits{half}")
                        wait_alone(pe, aux_free[bank], before + 1)
                    bank, ps = take(turn, j, "by_token")
                    for t in range(TILES):
                        mm = pe.transpose(ps[:, t * E:(t + 1) * E], logits_t[:, t * TILE:(t + 1) * TILE],
                                          ident[0:E, 0:E])
                    mm.then_inc(aux_full[bank], 1)

                def turn_gates(turn, j):
                    bank, ps = take(turn, j, "gates")
                    pe.wait_ge(gates_ready, RING * turn + j + 1)
                    for half in range(2):
                        mm = pe.transpose(ps[0:stack, half * TILE:(half + 1) * TILE],
                                          gate_parts[:, half * HALF:(half + 1) * HALF, :, :].rearrange(
                                              "p t s e -> p (t s e)"), ident[:])
                    mm.then_inc(aux_full[bank], 1)

                def bias_half(turn, j, half):
                    if half == 0:
                        gates, before = aux(turn, j, "gates")
                        pe.wait_ge(aux_free[gates], before + 1)
                    bank, ps = take(turn, j, f"bias{half}")
                    pe.matmul(ps[:], gate_t[:, half, :], b_stack[:], start=True, stop=True).then_inc(aux_full[bank], 1)

                def expert_tile(turn, j, t):
                    y, before = y_bank(turn, j, t)
                    wait(pe, dve_read[y], before)
                    wait(pe, act_read[y], before)
                    cols = slice(t * TILE, (t + 1) * TILE)
                    for tt, ws in ((t_hi, (e_hi, e_lo)), (t_lo, (e_hi,))):
                        for w in ws:
                            for b in range(2):
                                mm = pe.matmul(ps_y[y][b][:], tt[:, j % 2, cols],
                                               w[:, 4 * b:4 * b + 4, :].rearrange("p e c -> p (e c)"),
                                               start=(tt is t_hi and w is e_hi), stop=(tt is t_lo))
                    mm.then_inc(y_full, 1)

                def job(turn, j, i):
                    name = AUX_JOBS[i]
                    if name.startswith("turn"):
                        turn_half(turn, j, i)
                    elif name.startswith("logits"):
                        logits_half(turn, j, i - 2)
                    elif name == "by_token":
                        by_token(turn, j)
                    elif name == "gates":
                        turn_gates(turn, j)
                    else:
                        bias_half(turn, j, i - 6)

                for i in range(len(AUX_JOBS)):
                    job(0, 0, i)
                with pe.Fori(0, turns) as turn:
                    for j in range(RING):
                        for t in range(TILES):
                            expert_tile(turn, j, t)
                            for i in jobs_at(t):
                                job(turn, j + 1, i)

            @block.scalar
            def _(act):
                act.preload_act_table_set("natural_log_exp_and_others")

                def full(turn, j, name):
                    bank, before = aux(turn, j, name)
                    act.wait_ge(aux_full[bank], before + 1)
                    return bank, ps_a[bank]

                def normalise(turn, j, tiles):
                    n = RING * turn + j
                    act.wait_ge(scale_ready, n + 1)
                    for t in tiles:
                        last = act.activation(t_norm[:, j % 2, t, :], t_in[:, j % RING, t, :], ACT.Identity,
                                              scale=t_scale[:, j % 2, 0, t:t + 1], bias=t_scale[:, j % 2, 1, t:t + 1])
                    if TILES - 1 in tiles:
                        last.then_inc(norm_done, 1)

                def job(turn, j, i):
                    name = AUX_JOBS[i]
                    n = RING * turn + j
                    if name.startswith("turn"):
                        bank, ps = full(turn, j, name)
                        act.activation(t_hi[:, j % 2, i * 512:(i + 1) * 512], ps[:], ACT.Copy).then_inc(hi_done, 1)
                    elif name.startswith("logits"):
                        bank, ps = full(turn, j, name)
                        act.activation(logits_t[:, (i - 2) * 512:(i - 1) * 512], ps[0:E, :], ACT.Identity,
                                       bias=r_bias[:]).then_inc(aux_free[bank], 1)
                    elif name == "gates":
                        bank, ps = full(turn, j, name)
                        act.activation(gate_t[:].rearrange("p h t -> p (h t)"), ps[0:stack, 0:2 * TILE], ACT.Copy
                                       ).then_inc(aux_free[bank], 1)

                def gap_exponential(turn, j):
                    act.wait_ge(gap_ready, RING * turn + j + 1)
                    act.activation(gap[:, 1, :], gap[:, 0, :], ACT.Exp).then_inc(gap_exp, 1)

                def weigh(turn, j, t):
                    n = TILES * (RING * turn + j) + t
                    y, _ = y_bank(turn, j, t)
                    act.wait_ge(y_full, n + 1)
                    wait(act, summed[t % SUMS], sums_before(turn, j, t))
                    for e in range(ON_DVE, E):
                        last = act.activation(scaled[:, t % SUMS, e - ON_DVE, :],
                                              ps_y[y][1][:, (e - ON_DVE) * D:(e - ON_DVE + 1) * D], ACT.Copy,
                                              scale=gate[:, j % 2, t, e:e + 1])
                    last.then_inc(act_read[y], 1)

                normalise(0, 0, range(TILES))
                for i in range(len(AUX_JOBS)):
                    job(0, 0, i)
                    if AUX_JOBS[i] == "by_token":
                        gap_exponential(0, 0)
                normalise(0, 1, range(TILES))
                share = 3
                with act.Fori(0, turns) as turn:
                    for j in range(RING):
                        for t in range(TILES):
                            weigh(turn, j, t)
                            if t == CHOOSE_AT:
                                gap_exponential(turn, j + 1)
                            for i in jobs_at(t):
                                job(turn, j + 1, i)
                            first = share * (t - NORM_AT)
                            if 0 <= first < TILES:
                                normalise(turn, j + 2, range(first, min(first + share, TILES)))

            @block.vector
            def _(dve):
                def statistics(turn, j, tiles):
                    if 0 == tiles[0]:
                        wait(dve, scale_ready, RING * turn + j - 1)
                        dve.wait_ge(t_landed[j % RING], 16 * (turn + j // RING + 1))
                    for t in tiles:
                        dve.bn_stats(counts[:, j % 2, t, :], t_in[:, j % RING, t, :]).then_inc(counted, 1)

                def choose(turn, j, step):
                    n = RING * turn + j
                    before = GATE_STEPS * n
                    if step == 0:
                        bank, jobs = aux(turn, j, "by_token")
                        dve.wait_ge(aux_full[bank], jobs + 1)
                        dve.tensor_copy(logits[:].rearrange("p t e -> p (t e)"), ps_a[bank][:, 0:TILES * E]
                                        ).then_inc(aux_free[bank], 1)
                    elif step == 1:
                        bank, jobs = aux(turn, j, "by_token")
                        wait_alone(dve, aux_free[bank], jobs + 1)
                        for t in range(TILES):
                            last = dve.max(top[:, t, :], logits[:, t, :])
                        last.then_inc(gate_step, 1)
                    elif step == 2:
                        dve.wait_ge(gate_step, before + 1)
                        dve.tensor_tensor(gap[:, 0, :], top[:, :, 1], top[:, :, 0], ALU.subtract
                                          ).then_inc(gap_ready, 1)
                        for t in range(TILES):
                            last = dve.max_index(top_at[:, t, :], top[:, t, :], logits[:, t, :])
                        last.then_inc(gate_step, 1)
                    elif step == 3:
                        dve.wait_ge(gate_step, before + 2)
                        dve.tensor_copy(top_no[:], top_at[:, :, 0:TOP].rearrange("p t k -> p k t")
                                        ).then_inc(gate_step, 1)
                    elif step == 4:
                        dve.wait_ge(gate_step, before + 3)
                        for k in range(TOP):
                            dve.tensor_tensor(chosen[:, k, :, :], number[:], wide(top_no[:, k, :]), ALU.is_equal)
                    elif step == 5:
                        dve.wait_ge(gap_exp, n + 1)
                        dve.tensor_scalar(gap[:, 2, :], gap[:, 1, :], 1.0, None, ALU.add).then_inc(gate_step, 1)
                    elif step == 6:
                        dve.wait_ge(gate_step, before + 4)
                        dve.reciprocal(gap[:, 3, :], gap[:, 2, :]).then_inc(gate_step, 1)
                    elif step == 7:
                        dve.wait_ge(gate_step, before + 5)
                        dve.tensor_tensor(gate2[:], gap[:, 1, :], gap[:, 3, :], ALU.mult)
                        dve.tensor_tensor(chosen[:, 0, :, :], chosen[:, 0, :, :], wide(gap[:, 3, :]), ALU.mult
                                          ).then_inc(gate_step, 1)
                    elif step == 8:
                        dve.wait_ge(gate_step, before + 6)
                        dve.tensor_tensor(chosen[:, 1, :, :], chosen[:, 1, :, :], wide(gate2[:]), ALU.mult
                                          ).then_inc(gate_step, 1)
                    elif step == 9:
                        dve.wait_ge(gate_step, before + 7)
                        dve.tensor_tensor(gate[:, j % 2, :, :], chosen[:, 0, :, :], chosen[:, 1, :, :], ALU.add
                                          ).then_inc(gate_step, 1)
                    elif step == 10:
                        dve.wait_ge(gate_step, before + 8)
                        dve.tensor_copy(gate_cut[:], gate[:, j % 2, :, :]).then_inc(gate_step, 1)
                    else:
                        dve.wait_ge(gate_step, before + 9)
                        dve.tensor_copy(gate_parts[:, :, 0, :], gate_cut[:].bitcast(F32))
                        dve.tensor_copy(gate_parts[:, :, 2, :], gate_cut[:].bitcast(F32))
                        dve.tensor_tensor(gate_parts[:, :, 1, :], gate[:, j % 2, :, :], gate_cut[:].bitcast(F32),
                                          ALU.subtract).then_inc(gates_ready, 1)

                def wide(a):
                    return a.unsqueeze(2).broadcast_to([TILE, TILES, E])

                def job(turn, j, i):
                    name = AUX_JOBS[i]
                    n = RING * turn + j
                    bank, before = aux(turn, j, name)
                    if name.startswith("turn"):
                        dve.wait_ge(hi_done, 2 * n + i + 1)
                        cols = slice(i * 512, (i + 1) * 512)
                        dve.tensor_tensor(t_lo[:, j % 2, cols], ps_a[bank][:], t_hi[:, j % 2, cols].bitcast(F32),
                                          ALU.subtract).then_inc(aux_free[bank], 1)
                    elif name.startswith("bias"):
                        half = i - 6
                        tiles = slice(half * HALF, (half + 1) * HALF)
                        dve.wait_ge(aux_full[bank], before + 1)
                        dve.tensor_tensor(base[:, j % 2, tiles, :], ps_a[bank][:].rearrange("p (t c) -> p t c", t=HALF),
                                          t_in[:, j % RING, tiles, :], ALU.add).then_inc(aux_free[bank], 1)

                def weigh(turn, j, t, e):
                    n = TILES * (RING * turn + j) + t
                    y, _ = y_bank(turn, j, t)
                    if e == 0:
                        before = base[:, j % 2, t, :]
                        dve.wait_ge(y_full, n + 1)
                        wait(dve, summed[t % SUMS], sums_before(turn, j, t))
                        if t in (0, HALF):
                            bank, jobs = aux(turn, j, f"bias{t // HALF}")
                            dve.wait_ge(aux_free[bank], jobs + 1)
                    else:
                        before = part[:, t % SUMS, e - 1, :]
                        dve.wait_ge(sum_step, (ON_DVE - 1) * n + e)
                    ins = dve.scalar_tensor_tensor(
                        out=part[:, t % SUMS, e, :], in0=ps_y[y][0][:, e * D:(e + 1) * D],
                        scalar=gate[:, j % 2, t, e:e + 1], in1=before, op0=ALU.mult, op1=ALU.add)
                    if e < ON_DVE - 1:
                        ins.then_inc(sum_step, 1)
                    else:
                        ins.then_inc(dve_read[y], 1)

                statistics(0, 0, range(TILES))
                statistics(0, 1, range(TILES))
                statistics(0, 2, range(STATS_AHEAD))
                for i in range(len(AUX_JOBS)):
                    job(0, 0, i)
                    if AUX_JOBS[i] == "by_token":
                        for step in range(CHOOSE_STEPS):
                            choose(0, 0, step)
                with dve.Fori(0, turns) as turn:
                    for j in range(RING):
                        for t in range(TILES):
                            for e in range(ON_DVE):
                                weigh(turn, j, t, e)
                                if CHOOSE_AT <= t < CHOOSE_AT + CHOOSE_STEPS // ON_DVE:
                                    choose(turn, j + 1, ON_DVE * (t - CHOOSE_AT) + e)
                                elif t == 0 and e < 2:
                                    statistics(turn, j + 2, (STATS_AHEAD + e,))
                                elif t == TILES - 2 or t == TILES - 1 and e < 2:
                                    statistics(turn, j + 3, (ON_DVE * (t - TILES + 2) + e,))
                                elif t == 0:
                                    job(turn, j + 1, AUX_JOBS.index(f"turn{e - 2}"))
                                elif t == TILES - 1:
                                    job(turn, j + 1, AUX_JOBS.index(f"bias{e - 2}"))

            @block.gpsimd
            def _(pool):
                count = [0, None]

                def done(ins):
                    ins.then_inc(moe_step, 1)
                    count[0] += 1

                def settle(stand_alone=False):
                    turn = count[1]
                    (wait_alone if stand_alone else wait)(
                        pool, moe_step, count[0] if turn is None else count[0] + MOE_STEPS_A_TURN * turn)

                stat = [stat_tmp[:, i, :] for i in range(3)]

                def batch_variances(turn, j):
                    pool.wait_ge(counted, TILES * (RING * turn + j + 1))
                    wait(pool, scale_ready, RING * turn + j)
                    variances(pool, done, settle, counts[:, j % 2, :, :], stat, D, EPS_TOKEN)

                def batch_scales(turn, j):
                    rstd(pool, done, settle, stat, t_scale[:, j % 2, 0, :], t_scale[:, j % 2, 1, :], minus_half[:]
                         ).then_inc(scale_ready, 1)

                def steps_so_far():
                    return count[0] + MOE_STEPS_A_TURN * count[1]

                def add_pairs(turn, j, t):
                    s = scaled[:, t % SUMS, :, :]
                    y, before = y_bank(turn, j, t)
                    pool.wait_ge(act_read[y], before + 1)
                    done(pool.tensor_tensor(s[:, 0:2, :], s[:, 0:2, :], s[:, 2:4, :], ALU.add))
                    return steps_so_far()

                def add_halves(turn, j, t, paired):
                    s = scaled[:, t % SUMS, :, :]
                    pool.wait_ge(moe_step, paired)
                    done(pool.tensor_tensor(s[:, 0, :], s[:, 0, :], s[:, 1, :], ALU.add))
                    return steps_so_far()

                def add_dve_part(turn, j, t, halved):
                    pool.wait_ge(moe_step, halved)
                    y, before = y_bank(turn, j, t)
                    pool.wait_ge(dve_read[y], before + 1)
                    if t == 0:
                        wait(pool, out_stored[j % 2], 32 * (RING // 2 * turn + j // 2))
                    pool.tensor_tensor(t_out[:, j % 2, t, :], scaled[:, t % SUMS, 0, :], part[:, t % SUMS, ON_DVE - 1, :],
                                       ALU.add).then_inc(summed[t % SUMS], 1)

                for j in range(2):
                    batch_variances(0, j)
                    batch_scales(0, j)
                ahead = count[0]
                with pool.Fori(0, turns) as turn:
                    count[1] = turn
                    for j in range(RING):
                        halved = None
                        for t in range(TILES):
                            paired = add_pairs(turn, j, t)
                            if t > 0:
                                add_dve_part(turn, j, t - 1, halved)
                            halved = add_halves(turn, j, t, paired)
                            if t == SCALES_AT:
                                batch_variances(turn, j + 2)
                            elif t == SCALES_AT + 1:
                                batch_scales(turn, j + 2)
                        add_dve_part(turn, j, TILES - 1, halved)
                    assert count[0] == ahead + MOE_STEPS_A_TURN


_INS = ['x', 'L0_conv_Wq', 'L0_conv_Wk', 'L0_conv_Wv', 'L0_conv_ln_gamma', 'L0_conv_ln_beta',
        'L0_ffn_router_w', 'L0_ffn_router_b', 'L0_ffn_expert_w', 'L0_ffn_expert_b']
_OUT = (B, C, H, W)


def metaformer(nc, x, wq, wk, wv, gamma, beta, router_w, router_b, expert_w, expert_b, out):
    mixed = nc.dram_tensor("mixed", (B + 1, C, H, W), F32).ap()
    attention(nc, x, wq, wk, wv, gamma, beta, mixed)
    experts(nc, mixed, router_w, router_b, expert_w, expert_b, out)


def kernel(**inputs):
    import numpy as _np
    import concourse.bacc as _bacc
    from concourse import mybir as _mybir
    from concourse.bass_utils import run_bass_kernel_spmd as _run

    nc = _bacc.Bacc("TRN2", target_bir_lowering=False, num_devices=1)
    arrays, args = {}, []
    for name in _INS:
        a = _np.ascontiguousarray(inputs[name])
        arrays[f"in_{name}_dram"] = a
        args.append(nc.dram_tensor(f"in_{name}_dram", a.shape, _mybir.dt.from_np(a.dtype), kind="ExternalInput").ap())
    args.append(nc.dram_tensor("out_0_dram", _OUT, _mybir.dt.float32, kind="ExternalOutput").ap())
    metaformer(nc, *args)
    r = _run(nc, [arrays], core_ids=[0])
    return r.results[0]["out_0_dram"]
```
